# Optimizing a Trainium2 kernel written in Bass

```python
import numpy as np
import jax
import jax.numpy as jnp

def _softmax(x, axis=-1):
    return jax.nn.softmax(x, axis=axis)

def _gelu(x):
    return jax.nn.gelu(x, approximate=True)

def _silu(x):
    return jax.nn.silu(x)

def _sigmoid(x):
    return jax.nn.sigmoid(x)

def _layernorm(x, axis=-1, eps=1e-05):
    m = jnp.mean(x, axis=axis, keepdims=True)
    v = jnp.var(x, axis=axis, keepdims=True)
    return (x - m) / jnp.sqrt(v + eps)

def _scatter_add(tgt, idx, src, axis=0):
    return tgt.at[idx].add(src)

def _segment_sum(src, seg, n):
    return jax.ops.segment_sum(src, seg, n)
kernel_name = 'mk_xattn_ffn_d1_seqx_r4_b0bbc6'

def setup_inputs(seed: int=0):
    np.random.seed(seed)
    _w = jnp.asarray

    def _rec_inputs():
        import jax
        import jax.numpy as jnp
        _rk = jax.random.key(seed)
        x = -0.000125 + 0.9999 * jax.random.normal(jax.random.fold_in(_rk, 1), (16, 128, 1024), jnp.float32)
        _lenS = 128 - jax.random.randint(jax.random.fold_in(_rk, 7), (16,), 0, max(1, 128 // 4) + 1, jnp.int32)
        _lenS2 = 128 - jax.random.randint(jax.random.fold_in(_rk, 8), (16,), 0, max(1, 128 // 4) + 1, jnp.int32)
        _ctx_4096P = jax.random.normal(jax.random.fold_in(_rk, 11), (16, 16, 1024), jnp.float32)
        _ctx_4096c = jax.random.dirichlet(jax.random.fold_in(_rk, 511), 0.3 * jnp.ones((16,), jnp.float32), (16, 128))
        _ctx_4096t = jnp.einsum('bsk,bkd->bsd', _ctx_4096c, _ctx_4096P)
        _ctx_4096t = _ctx_4096t * jax.lax.rsqrt(jnp.mean(jnp.square(_ctx_4096t)) + 1e-12) * 0.953939
        ctx_4096 = -1.52775e-05 + 0.999936 * (_ctx_4096t + 0.3 * jax.random.normal(jax.random.fold_in(_rk, 611), (16, 128, 1024), jnp.float32))
        return (x, ctx_4096)
    x, ctx_4096 = _rec_inputs()

    def _L0_xattn_setup():
        import jax, jax.numpy as jnp
        import numpy as np
        NUM_HEADS = 8

        def _proj(W, b, x):
            return jnp.einsum('oi,bil->bol', W, x) + b[:, None]
        key = jax.random.key(seed)
        ks = jax.random.split(key, 11)
        B, D, L = (16, 128, 1024)
        s = 1.0 / np.sqrt(D).astype(np.float32)
        return {'x_query': jax.random.normal(ks[0], (B, D, L), jnp.float32), 'x_key': jax.random.normal(ks[1], (B, D, L), jnp.float32), 'x_value': jax.random.normal(ks[2], (B, D, L), jnp.float32), 'Wq': jax.random.normal(ks[3], (D, D), jnp.float32) * s, 'bq': jax.random.normal(ks[4], (D,), jnp.float32) * 0.01, 'Wk': jax.random.normal(ks[5], (D, D), jnp.float32) * s, 'bk': jax.random.normal(ks[6], (D,), jnp.float32) * 0.01, 'Wv': jax.random.normal(ks[7], (D, D), jnp.float32) * s, 'bv': jax.random.normal(ks[8], (D,), jnp.float32) * 0.01, 'Wo': jax.random.normal(ks[9], (D, D), jnp.float32) * s, 'bo': jax.random.normal(ks[10], (D,), jnp.float32) * 0.01}
    _L0_xattn_all = _L0_xattn_setup()
    _L0_xattn_in = {k: v for k, v in _L0_xattn_all.items() if k in ('Wq', 'bq', 'Wk', 'bk', 'Wv', 'bv', 'Wo', 'bo')}
    del _L0_xattn_all

    def _L0_ffn_setup():
        import jax, jax.numpy as jnp
        import numpy as np
        GROUP = 64

        def dequant_q40(w, s, out_features, in_features):
            msb = w >> 4
            lsb = (w & 15 ^ 8) - 8
            g = jnp.concatenate([msb, lsb], axis=1).reshape(-1, GROUP)
            deq = g.astype(s.dtype) * s[:, None]
            return deq.reshape(out_features, in_features)
        key = jax.random.key(seed)
        ks = jax.random.split(key, 7)
        dim, hidden = (1024, 2752)
        B, S = (2, 512)

        def packed(k, din, dout):
            return jax.random.randint(k, (din * dout // GROUP // 2, GROUP), -128, 128, dtype=jnp.int32)

        def scales(k, din, dout):
            return (jax.random.uniform(k, (din * dout // GROUP,), dtype=jnp.float32) + 0.5) * 0.01
        x = jax.random.normal(ks[0], (B, S, dim), dtype=jnp.float32)
        w1 = packed(ks[1], dim, hidden)
        s1 = scales(ks[2], dim, hidden)
        w2 = packed(ks[3], hidden, dim)
        s2 = scales(ks[4], hidden, dim)
        w3 = packed(ks[5], dim, hidden)
        s3 = scales(ks[6], dim, hidden)
        return {'x': x, 'w1': w1, 's1': s1, 'w2': w2, 's2': s2, 'w3': w3, 's3': s3}
    _L0_ffn_all = _L0_ffn_setup()
    _L0_ffn_in = {k: v for k, v in _L0_ffn_all.items() if k in ('w1', 's1', 'w2', 's2', 'w3', 's3')}
    del _L0_ffn_all
    return {'x': x, 'ctx_4096': ctx_4096, 'L0_xattn_Wq': _L0_xattn_in['Wq'], 'L0_xattn_bq': _L0_xattn_in['bq'], 'L0_xattn_Wk': _L0_xattn_in['Wk'], 'L0_xattn_bk': _L0_xattn_in['bk'], 'L0_xattn_Wv': _L0_xattn_in['Wv'], 'L0_xattn_bv': _L0_xattn_in['bv'], 'L0_xattn_Wo': _L0_xattn_in['Wo'], 'L0_xattn_bo': _L0_xattn_in['bo'], 'L0_ffn_w1': _L0_ffn_in['w1'], 'L0_ffn_s1': _L0_ffn_in['s1'], 'L0_ffn_w2': _L0_ffn_in['w2'], 'L0_ffn_s2': _L0_ffn_in['s2'], 'L0_ffn_w3': _L0_ffn_in['w3'], 'L0_ffn_s3': _L0_ffn_in['s3']}

def reference(x, ctx_4096, L0_xattn_Wq, L0_xattn_bq, L0_xattn_Wk, L0_xattn_bk, L0_xattn_Wv, L0_xattn_bv, L0_xattn_Wo, L0_xattn_bo, L0_ffn_w1, L0_ffn_s1, L0_ffn_w2, L0_ffn_s2, L0_ffn_w3, L0_ffn_s3):
    import jax
    import jax.numpy as jnp

    def _L0_xattn_ref(x_query, x_key, x_value, Wq, bq, Wk, bk, Wv, bv, Wo, bo):
        import jax, jax.numpy as jnp
        import numpy as np
        NUM_HEADS = 8

        def _proj(W, b, x):
            return jnp.einsum('oi,bil->bol', W, x) + b[:, None]
        B, D, L = x_query.shape
        h = NUM_HEADS
        Lh = L // h
        q = _proj(Wq, bq, x_query)
        k = _proj(Wk, bk, x_key)
        v = _proj(Wv, bv, x_value)
        qh = q.reshape(B, D, h, Lh).transpose(2, 0, 1, 3)
        kh = k.reshape(B, D, h, Lh).transpose(2, 0, 1, 3)
        vh = v.reshape(B, D, h, Lh).transpose(2, 0, 1, 3)
        scale = 1.0 / jnp.sqrt(jnp.asarray(Lh, x_query.dtype))
        scores = jnp.einsum('hbdk,hbek->hbde', qh, kh) * scale
        p = jax.nn.softmax(scores, axis=-1)
        xh = jnp.einsum('hbde,hbek->hbdk', p, vh)
        x = xh.transpose(1, 2, 0, 3).reshape(B, D, L)
        return _proj(Wo, bo, x)

    def _L0_ffn_ref(x, w1, s1, w2, s2, w3, s3):
        import jax, jax.numpy as jnp
        import numpy as np
        GROUP = 64

        def dequant_q40(w, s, out_features, in_features):
            msb = w >> 4
            lsb = (w & 15 ^ 8) - 8
            g = jnp.concatenate([msb, lsb], axis=1).reshape(-1, GROUP)
            deq = g.astype(s.dtype) * s[:, None]
            return deq.reshape(out_features, in_features)
        dim = x.shape[-1]
        hidden = w1.shape[0] * w1.shape[1] * 2 // dim
        W1 = dequant_q40(w1, s1, hidden, dim)
        W3 = dequant_q40(w3, s3, hidden, dim)
        W2 = dequant_q40(w2, s2, dim, hidden)
        a = jnp.einsum('bsd,hd->bsh', x, W1)
        b = jnp.einsum('bsd,hd->bsh', x, W3)
        h = jax.nn.silu(a) * b
        return jnp.einsum('bsh,dh->bsd', h, W2)
    x = x + _L0_xattn_ref(_layernorm(x, axis=-1), ctx_4096, ctx_4096, L0_xattn_Wq, L0_xattn_bq, L0_xattn_Wk, L0_xattn_bk, L0_xattn_Wv, L0_xattn_bv, L0_xattn_Wo, L0_xattn_bo)
    x = x + _L0_ffn_ref(_layernorm(x, axis=-1), L0_ffn_w1, L0_ffn_s1, L0_ffn_w2, L0_ffn_s2, L0_ffn_w3, L0_ffn_s3)
    return x

_drawn_inputs = setup_inputs


def setup_inputs(seed=0):
    import zlib

    import numpy as np

    out = dict(_drawn_inputs(seed))
    spreads = {}
    factors = {'L0_xattn_bq': 8.0, 'L0_xattn_bk': 8.0, 'L0_xattn_bv': 36.294, 'L0_xattn_bo': 8.0}
    for name, (base, spread) in spreads.items():
        noise = np.random.default_rng([zlib.crc32(name.encode()), seed]).standard_normal(out[name].shape)
        drawn = base * np.exp(spread * noise) if base else spread * noise
        out[name] = jnp.asarray(drawn.astype(out[name].dtype))
    for name, factor in factors.items():
        out[name] = (out[name] * factor).astype(out[name].dtype)
    return out
```

```python
import concourse.bass as bass
from concourse import mybir
from contextlib import ExitStack


def bass_xattn_ffn_kernel(nc, x, ctx_in, wq, bq, wk, bk, wv, bv, wo, bo, w1, s1, w2, s2, w3, s3, out):
    fp32, fp16, i32 = mybir.dt.float32, mybir.dt.float16, mybir.dt.int32
    ALU, ACT, AX = mybir.AluOpType, mybir.ActivationFunctionType, mybir.AxisListType

    B, D, L = x.shape
    P = 128
    H = 8
    LH = L // H
    HH = H // 2
    HL = HH * LH
    G = 64
    F = w1.shape[0] * 2 * G // L
    NT = -(-F // P)
    LAST = F - (NT - 1) * P
    K = L // P
    T = B * D
    TW = 512
    TS = T // TW
    TOK = TW // P
    YG = TOK * L // 512
    GT = TS * YG
    ROWG = F // G
    MB = L // (2 * P)
    EPS = 1e-5
    SCALE = float(LH) ** -0.5
    XS = 10
    WS = 11
    HSH = 13
    TINY = 2.0 ** -40

    with ExitStack() as stack:
        def sb(name, shape, dt):
            return stack.enter_context(nc.sbuf_tensor(name, shape, dt))

        def sem(name):
            return stack.enter_context(nc.semaphore(name))

        acc = sb("acc", [P, B, L], fp32)
        xT_hi = sb("xT_hi", [P, K, T], fp16)
        xT_lo = sb("xT_lo", [P, K, T], fp16)
        shared = sb("shared", [P, 10 * L], fp32)
        w13_even = sb("w13_even", [P, 4 * L], fp16)
        raw = sb("raw", [P, 2, 12 * G], i32)
        q_int = sb("q_int", [P, 2, L], i32)
        wn_hi = sb("wn_hi", [P, 2, L], fp16)
        wn_lo = sb("wn_lo", [P, 2, L], fp16)
        s1_sb = sb("s1_sb", [P, NT, 2 * K], fp32)
        s3_sb = sb("s3_sb", [P, NT, 2 * K], fp32)
        s2_sb = sb("s2_sb", [P, 2 * MB, ROWG + 1], fp32)
        ident = sb("ident", [P, P], fp32)
        ident16 = sb("ident16", [P, P], fp16)
        wT = sb("wT", [P, 4, P], fp32)
        bq_row = sb("bq_row", [P, P], fp32)
        bk_row = sb("bk_row", [P, P], fp32)
        bv_col = sb("bv_col", [P, 1], fp32)
        bo_col = sb("bo_col", [P, 1], fp32)
        neg_half = sb("neg_half", [P, 1], fp32)
        smax = sb("smax", [P, 3], fp32)
        smax_all = sb("smax_all", [P, 3], fp32)
        pow2 = sb("pow2", [P, 3], fp32)
        winv = sb("winv", [P, 3], fp32)
        prod = sb("prod", [P, 1], fp32)
        a_scale = sb("a_scale", [P, 1], fp32)
        h_scale = sb("h_scale", [P, 1], fp32)
        y_scale = sb("y_scale", [P, 1], fp32)
        stats1 = sb("stats1", [P, 2, 6], fp32)
        stats2 = sb("stats2", [P, 2, 6], fp32)
        mv1 = sb("mv1", [P, 2], fp32)
        mv2 = sb("mv2", [P, 2], fp32)
        ln1 = sb("ln1", [P, 2], fp32)
        ln2 = sb("ln2", [P, 2], fp32)
        rstd1 = sb("rstd1", [P, 1], fp32)
        rstd2 = sb("rstd2", [P, 1], fp32)
        gate_dve = sb("gate_dve", [P, 1], fp32)
        gate_pool = sb("gate_pool", [P, 3], fp32)
        nmax = sb("nmax", [P, H], fp32)
        rsum = sb("rsum", [P, H], fp32)
        rinv = sb("rinv", [P, H], fp32)

        def part(n, count, dt=fp32):
            view = shared[:, n * L:(n + count) * L]
            return view if dt is fp32 else view.bitcast(dt)

        ctx = [part(0, 1), part(1, 1)]
        vbuf = [part(2, 1), part(3, 1)]
        xn, qT, kT, prob, wop, x2 = (part(n, 1) for n in range(4, 10))
        w_nat = part(9, 1)
        h_hi = [part(0, 1, fp16), part(1, 1, fp16)]
        h_lo = [part(2, 1, fp16), part(3, 1, fp16)]
        silu_sb = [part(4, 1)[:, 0:TW], part(4, 1)[:, TW:2 * TW]]
        h32 = [part(5, 1)[:, 0:TW], part(5, 1)[:, TW:2 * TW]]
        w13 = [w13_even[:, :], part(6, 2, fp16)]
        w2T = [part(8, 1, fp16), part(9, 1, fp16)]

        def w13_at(slot, which, half):
            o = (2 * which + half) * L
            return w13[slot][:, o:o + L]

        def w2_at(slot, half):
            return w2T[slot][:, half * L:(half + 1) * L]

        bank = [stack.enter_context(nc.psum_tensor(f"bank{n}", [P, 512], fp32)) for n in range(8)]
        q_ps, k_ps, v_ps, s_ps = bank[0:2], bank[2:4], bank[4:6], bank[6:8]
        wop_ps, y_ps, t_ps = bank[0:2], bank[2:4], bank[4:6]
        a_ps, b_ps, o_ps = [bank[0], bank[2]], [bank[1], bank[3]], [bank[4], bank[5]]
        wt_ps = [bank[6][:, :].bitcast(fp16), bank[7][:, :].bitcast(fp16)]

        s_zero = sem("s_zero")
        s_scales = sem("s_scales")
        s_proj_in = sem("s_proj_in")
        s_ident = sem("s_ident")
        s_projT = sem("s_projT")
        s_proj = sem("s_proj")
        s_bias = sem("s_bias")
        s_smax = sem("s_smax")
        s_smax_all = sem("s_smax_all")
        s_pow = sem("s_pow")
        s_sc = sem("s_sc")
        x_in = [sem("x_in0"), sem("x_in1")]
        c_in = [sem("c_in0"), sem("c_in1")]
        s_bn1, s_mv1, s_ln1, s_rstd1, s_xn = (sem(n) for n in ("s_bn1", "s_mv1", "s_ln1", "s_rstd1", "s_xn"))
        s_bn2, s_mv2, s_ln2, s_rstd2, s_x2 = (sem(n) for n in ("s_bn2", "s_mv2", "s_ln2", "s_rstd2", "s_x2"))
        s_x1c, s_x2c = sem("s_x1c"), sem("s_x2c")
        s_q, s_k, s_v = sem("s_q"), sem("s_k"), sem("s_v")
        s_qe, s_ke, s_ve = sem("s_qe"), sem("s_ke"), sem("s_ve")
        s_score = sem("s_score")
        s_nmax = sem("s_nmax")
        s_exp = sem("s_exp")
        s_rinv = sem("s_rinv")
        s_prob = sem("s_prob")
        s_wop = sem("s_wop")
        s_wope = sem("s_wope")
        s_att = sem("s_att")
        s_res = sem("s_res")
        s_xT = sem("s_xT")
        s_xhi, s_xlo = sem("s_xhi"), sem("s_xlo")
        raw_in = [sem("raw_in0"), sem("raw_in1")]
        s_unp = sem("s_unp")
        s_wf, s_whi, s_wlo = sem("s_wf"), sem("s_whi"), sem("s_wlo")
        s_wT = sem("s_wT")
        s_wTe = sem("s_wTe")
        s_ab = sem("s_ab")
        s_silu, s_h, s_hhi, s_hlo = sem("s_silu"), sem("s_h"), sem("s_hhi"), sem("s_hlo")
        s_y = sem("s_y")
        s_acc = sem("s_acc")
        s_out = sem("s_out")

        def after(eng, s, count):
            if not (type(count) is int and count <= 0):
                eng.wait_ge(s, count)

        def num(at):
            return 2 * at[0] + at[1]

        def nxt(at):
            return (at[0], 1) if at[1] == 0 else (at[0] + 1, 0)

        def prv(at):
            return (at[0], 0) if at[1] == 1 else (at[0] - 1, 1)

        def mat(at, m):
            return 3 * num(at) + m, (3 * at[1] + m) % 2, 3 * at[0] + (3 * at[1] + m) // 2

        w1_rows = w1.rearrange("(h c) j -> h c j", c=K)
        w3_rows = w3.rearrange("(h c) j -> h c j", c=K)
        w2_rows = w2.rearrange("(m p r) j -> p m r j", p=P, r=ROWG)

        tiles = range(NT)
        block = stack.enter_context(nc.Block())

        @block.sync
        def _(sp):
            with nc.allow_non_contiguous_dma(reason="biases, one value per partition, once"):
                for n, w in enumerate((wq, wk, wv, wo)):
                    sp.dma_start(w_nat[:, n * P:(n + 1) * P], w).then_inc(s_proj_in, 16)
                sp.dma_start(bq_row[:, :], bq.rearrange("(a o) -> a o", a=1).to_broadcast([P, P])).then_inc(s_proj_in, 16)
                sp.dma_start(bk_row[:, :], bk.rearrange("(a o) -> a o", a=1).to_broadcast([P, P])).then_inc(s_proj_in, 16)
                sp.dma_start(bv_col[:, :], bv.rearrange("(o a) -> o a", a=1)).then_inc(s_proj_in, 16)
                sp.dma_start(bo_col[:, :], bo.rearrange("(o a) -> o a", a=1)).then_inc(s_proj_in, 16)

            def load_batch(at):
                b = num(at)
                after(sp, s_mv1, b - 1)
                sp.dma_start(acc[:, bass.ds(b, 1), :], x[bass.ds(b, 1)].rearrange("b s l -> s b l")).then_inc(x_in[at[1]], 16)
                after(sp, s_v, 2 * (b - 1))
                sp.dma_start(ctx[at[1]], ctx_in[bass.ds(b, 1)].rearrange("b s l -> s (b l)")).then_inc(c_in[at[1]], 16)

            load_batch((0, 0))
            load_batch((0, 1))

            sp.wait_ge(s_zero, 3)
            full = (NT - 1) * P
            with nc.allow_non_contiguous_dma(reason="scales, once"):
                for s, s_sb in ((s1, s1_sb), (s3, s3_sb)):
                    rows = s.rearrange("(h g) -> h g", g=2 * K)
                    sp.dma_start(s_sb[:, 0:NT - 1, :], rows[0:full].rearrange("(i p) g -> p i g", p=P)).then_inc(s_scales, 16)
                    sp.dma_start(s_sb[0:LAST, NT - 1, :], rows[full:F]).then_inc(s_scales, 16)
                pairs = s2.rearrange("(m p r k) -> m p r k", p=P, r=2, k=ROWG)
                for m in range(MB):
                    sp.dma_start(s2_sb[:, 2 * m:2 * m + 2, 0:ROWG], pairs[m]).then_inc(s_scales, 16)

            def load_weights(at, m):
                n, slot, _ = mat(at, m)
                i = num(at)
                dst = raw[:, slot, :]
                after(sp, s_unp, n - 1)
                if m < 2:
                    src = w1_rows if m == 0 else w3_rows
                    d = dst[:, 0:K * G].rearrange("p (c j) -> p c j", c=K)
                    half = K // 2
                    if type(i) is int and i == NT - 1:
                        for c in (0, half):
                            sp.dma_start(d[0:LAST, c:c + half, :], src[i * P:F, c:c + half, :]).then_inc(raw_in[slot], 16)
                    else:
                        for c in (0, half):
                            sp.dma_start(d[:, c:c + half, :], src[bass.ds(i * P, P), c:c + half, :]).then_inc(raw_in[slot], 16)
                else:
                    d = dst.rearrange("p (m r j) -> p m r j", m=MB, r=3)
                    first = ROWG // 2 + i
                    sp.dma_start(d[:, :, 0:1, :], w2_rows[:, :, bass.ds(i, 1), :]).then_inc(raw_in[slot], 16)
                    if type(i) is int and i == NT - 1:
                        sp.dma_start(d[:, :, 1:2, :], w2_rows[:, :, first:first + 1, :]).then_inc(raw_in[slot], 16)
                    else:
                        sp.dma_start(d[:, :, 1:3, :], w2_rows[:, :, bass.ds(first, 2), :]).then_inc(raw_in[slot], 16)

            load_weights((0, 0), 0)
            load_weights((0, 0), 1)
            with sp.Fori(1, B // 2) as u:
                load_batch((u, 0))
                load_batch((u, 1))
            load_weights((0, 0), 2)
            with sp.Fori(0, (NT - 2) // 2) as u:
                for at in ((u, 1), (u + 1, 0)):
                    for m in range(3):
                        load_weights(at, m)
            for m in range(3):
                load_weights(((NT - 1) // 2, 1), m)

            with sp.Fori(0, B) as b:
                sp.wait_ge(s_acc, GT * (NT - 1) + 2 * (b + 1))
                sp.dma_start(out[bass.ds(b, 1)].rearrange("b s l -> s b l"), acc[:, bass.ds(b, 1), :]).then_inc(s_out, 16)
            sp.wait_ge(s_out, 16 * B)

        @block.gpsimd
        def _(pool):
            nc.gpsimd.memset(s1_sb[:, :, :], 0.0).then_inc(s_zero, 1)
            nc.gpsimd.memset(s3_sb[:, :, :], 0.0).then_inc(s_zero, 1)
            nc.gpsimd.memset(s2_sb[:, :, :], 0.0).then_inc(s_zero, 1)
            nc.gpsimd.memset(neg_half[:, :], -0.5)
            nc.gpsimd.memset(ident16[:, :], 0.0).then_inc(s_ident, 1)
            nc.gpsimd.memset(ident[:, :], 0.0).then_inc(s_ident, 1)
            pool.wait_ge(s_ident, 2)
            for m in (ident, ident16):
                nc.gpsimd.affine_select(out=m[:, :], in_=m[:, :], compare_op=ALU.not_equal, fill=1.0, base=0,
                                        pattern=[[-1, P]], channel_multiplier=1).then_inc(s_ident, 1)

            def gate(site):
                nc.gpsimd.tensor_tensor(gate_pool[:, site:site + 1], neg_half[:, :], neg_half[:, :], ALU.add)

            def norm(site, b, s_ln, ln, s_copied, s_rstd, rstd, src, dst, s_done, s_free, free):
                after(pool, s_free, free)
                after(pool, s_ln, 2 * (b + 1))
                nc.gpsimd.tensor_tensor(rstd[:, :], ln[:, 1:2], neg_half[:, :], ALU.pow).then_inc(s_rstd, 1)
                nc.gpsimd.tensor_copy(dst.rearrange("p (a l) -> p a l", a=1), src).then_inc(s_copied, 1)
                pool.wait_ge(s_copied, b + 1)
                pool.wait_ge(s_rstd, b + 1)
                gate(site)
                nc.gpsimd.tensor_scalar(dst, dst, ln[:, 0:1], rstd[:, 0:1], ALU.add, ALU.mult).then_inc(s_done, 1)

            def norm1(at):
                b = num(at)
                norm(0, b, s_ln1, ln1, s_x1c, s_rstd1, rstd1, x_of(b), xn, s_xn, s_q, 2 * b)

            def norm2(at):
                b = num(at)
                norm(1, b, s_ln2, ln2, s_x2c, s_rstd2, rstd2, x_of(b), x2, s_x2, s_xT, 2 * b)

            def x_of(b):
                return acc[:, bass.ds(b, 1), :]

            def scale_prob(at):
                b = num(at)
                for hf in range(2):
                    pool.wait_ge(s_rinv, 2 * b + hf + 1)
                    p = prob[:, hf * HL:(hf + 1) * HL].rearrange("p (h e) -> p h e", h=HH)
                    r = rinv[:, hf * HH:(hf + 1) * HH].unsqueeze(2).to_broadcast([P, HH, LH])
                    nc.gpsimd.tensor_tensor(p, p, r, ALU.mult).then_inc(s_prob, 1)

            def att_step(at, ahead=True):
                scale_prob(at)
                if ahead:
                    norm1(nxt(nxt(at)))
                norm2(at)

            def split(at, m):
                n, slot, _ = mat(at, m)
                f = q_int[:, slot, :].bitcast(fp32)
                pool.wait_ge(s_wf, n + 1)
                after(pool, s_wT, 2 * (n - 1))
                gate(2)
                nc.gpsimd.tensor_copy(wn_hi[:, slot, :], f).then_inc(s_whi, 1)
                pool.wait_ge(s_whi, n + 1)
                nc.gpsimd.tensor_tensor(wn_lo[:, slot, :], f, wn_hi[:, slot, :], ALU.subtract).then_inc(s_wlo, 1)

            def h_low(at, t):
                n = TS * num(at) + t
                o = t * TW
                pool.wait_ge(s_hhi, n + 1)
                nc.gpsimd.tensor_tensor(h_lo[at[1]][:, o:o + TW], h32[t % 2], h_hi[at[1]][:, o:o + TW],
                                        ALU.subtract).then_inc(s_hlo, 1)

            def ffn_step(at, ahead=True):
                for t in range(TS):
                    if ahead and t < 3:
                        split(nxt(at), t)
                    h_low(at, t)

            norm1((0, 0))
            pool.wait_ge(s_smax, 3)
            nc.gpsimd.partition_all_reduce(smax_all[:, :], smax[:, :], P, bass.bass_isa.ReduceOp.max).then_inc(s_smax_all, 1)
            norm1((0, 1))
            att_step((0, 0))
            with pool.Fori(0, B // 2 - 2) as u:
                att_step((u, 1))
                att_step((u + 1, 0))
            att_step((B // 2 - 2, 1))
            split((0, 0), 0)
            att_step((B // 2 - 1, 0), ahead=False)
            split((0, 0), 1)
            att_step((B // 2 - 1, 1), ahead=False)
            split((0, 0), 2)
            ffn_step((0, 0))
            ffn_step((0, 1))
            with pool.Fori(1, NT // 2 - 1) as u:
                ffn_step((u, 0))
                ffn_step((u, 1))
            ffn_step((NT // 2 - 1, 0))
            ffn_step(((NT - 1) // 2, 1), ahead=False)

        @block.scalar
        def _(act):
            def copy_v(at):
                b = num(at)
                for hf in range(2):
                    act.wait_ge(s_v, 2 * b + hf + 1)
                    after(act, s_att, 2 * (b - 1))
                    nc.scalar.activation(vbuf[at[1]][:, hf * HL:(hf + 1) * HL], v_ps[hf][:, :], ACT.Identity,
                                         bias=bv_col[:, 0:1]).then_inc(s_ve, 1)

            def exps(at):
                b = num(at)
                for h in range(H):
                    hf, o = h // HH, (h % HH) * LH
                    if h % HH == 0:
                        act.wait_ge(s_nmax, 2 * b + hf + 1)
                        after(act, s_wop, 2 * b)
                        after(act, s_rinv, 2 * b)
                    nc.scalar.activation(prob[:, h * LH:(h + 1) * LH], s_ps[hf][:, o:o + LH], ACT.Exp,
                                         bias=nmax[:, h:h + 1], accum_out=rsum[:, h:h + 1]).then_inc(s_exp, 1)

            def copy_wop(at):
                b = num(at)
                for hf in range(2):
                    act.wait_ge(s_wop, 2 * b + hf + 1)
                    after(act, s_att, 2 * b)
                    nc.scalar.activation(wop[:, hf * HL:(hf + 1) * HL], wop_ps[hf][:, :], ACT.Copy).then_inc(s_wope, 1)

            def x_high(at):
                b = num(at)
                for hf in range(2):
                    act.wait_ge(s_xT, 2 * b + hf + 1)
                    nc.scalar.activation(xT_hi[:, hf * K // 2:(hf + 1) * K // 2, bass.ds(b * D, D)],
                                         t_ps[hf][:, :].rearrange("p (k s) -> p k s", s=D), ACT.Copy).then_inc(s_xhi, 1)

            def att_step(at, first=False, last=False):
                exps(at)
                if not last:
                    copy_v(nxt(at))
                if not first:
                    x_high(prv(at))
                copy_wop(at)

            def weight_slot(at, m):
                n, _, _ = mat(at, m)
                i = num(at)
                for half in range(2):
                    act.wait_ge(s_wT, 2 * n + half + 1)
                    src = wt_ps[half]
                    if m < 2:
                        after(act, s_ab, TS * (i - 1))
                        dst = w13_at(at[1], m, half)
                    else:
                        after(act, s_y, GT * (i - 1))
                        dst = w2_at(at[1], half).rearrange("p (m c r) -> p m r c", m=MB, r=2)
                        src = src.rearrange("p (m r c) -> p m r c", m=MB, r=2)
                    nc.scalar.activation(dst, src, ACT.Copy).then_inc(s_wTe, 1)

            def ffn_step(at, ahead=True):
                for t in range(TS):
                    n = TS * num(at) + t
                    act.wait_ge(s_ab, n + 1)
                    nc.scalar.activation(silu_sb[t % 2], a_ps[t % 2][:, :], ACT.Silu, scale=a_scale[:, 0:1]).then_inc(s_silu, 1)
                    if t == 0:
                        weight_slot(at, 2)
                    elif t < 3 and ahead:
                        weight_slot(nxt(at), t - 1)
                    act.wait_ge(s_h, n + 1)
                    after(act, s_y, GT * (num(at) - 1))
                    nc.scalar.activation(h_hi[at[1]][:, t * TW:(t + 1) * TW], h32[t % 2], ACT.Copy).then_inc(s_hhi, 1)

            act.wait_ge(s_projT, 4)
            for n in range(4):
                nc.scalar.activation(wT[:, n, :], bank[6][:, n * P:(n + 1) * P], ACT.Copy).then_inc(s_proj, 1)
            act.wait_ge(s_proj_in, 16 * 8)
            copy_v((0, 0))
            att_step((0, 0), first=True)
            with act.Fori(0, B // 2 - 1) as u:
                att_step((u, 1))
                att_step((u + 1, 0))
            att_step((B // 2 - 1, 1), last=True)
            x_high((B // 2 - 1, 1))
            weight_slot((0, 0), 0)
            weight_slot((0, 0), 1)
            act.wait_ge(s_pow, 8)
            ffn_step((0, 0))
            ffn_step((0, 1))
            with act.Fori(1, NT // 2 - 1) as u:
                ffn_step((u, 0))
                ffn_step((u, 1))
            ffn_step((NT // 2 - 1, 0))
            ffn_step(((NT - 1) // 2, 1), ahead=False)

        @block.tensor
        def _(pe):
            def cols(n, w=P):
                return slice(n * w, (n + 1) * w)

            def project(at):
                b = num(at)
                pe.wait_ge(s_xn, b + 1)
                pe.wait_ge(c_in[at[1]], 16 * (at[0] + 1))
                for hf in range(2):
                    after(pe, s_wope, 2 * (b - 2) + hf + 1)
                    for h in range(HH):
                        mm = nc.tensor.matmul(q_ps[hf][:, cols(h)], xn[:, cols(hf * HH + h)], wT[:, 0, :], start=True, stop=True)
                    mm.then_inc(s_q, 1)
                for hf in range(2):
                    after(pe, s_res, 2 * (b - 2) + hf + 1)
                    for h in range(HH):
                        mm = nc.tensor.matmul(k_ps[hf][:, cols(h)], ctx[at[1]][:, cols(hf * HH + h)], wT[:, 1, :], start=True, stop=True)
                    mm.then_inc(s_k, 1)
                for hf in range(2):
                    after(pe, s_ve, 2 * (b - 1) + hf + 1)
                    after(pe, s_xlo, 2 * (b - 3) + hf + 1)
                    nc.tensor.matmul(v_ps[hf][:, :], wT[:, 2, :], ctx[at[1]][:, cols(hf, HL)], start=True, stop=True).then_inc(s_v, 1)

            def scores(at):
                b = num(at)
                for hf in range(2):
                    pe.wait_ge(s_qe, 2 * b + hf + 1)
                    pe.wait_ge(s_ke, 2 * b + hf + 1)
                    after(pe, s_exp, H * (b - 1) + HH * (hf + 1))
                    for h in range(HH):
                        c = cols(hf * HH + h)
                        mm = nc.tensor.matmul(s_ps[hf][:, cols(h)], qT[:, c], kT[:, c], start=True, stop=True)
                    mm.then_inc(s_score, 1)

            def turn_x(at, v_next):
                b = num(at)
                pe.wait_ge(s_x2, b + 1)
                for hf in range(2):
                    if v_next:
                        pe.wait_ge(s_ve, 2 * (b + 2) + hf + 1)
                    else:
                        after(pe, s_xlo, 2 * (b - 1) + hf + 1)
                    for k in range(K // 2):
                        mm = nc.tensor.transpose(t_ps[hf][:, cols(k)], x2[:, cols(hf * K // 2 + k)], ident[:, :])
                    mm.then_inc(s_xT, 1)

            def wo_prob(at, last):
                b = num(at)
                for hf in range(2):
                    pe.wait_ge(s_prob, 2 * b + hf + 1)
                    if not last:
                        pe.wait_ge(s_qe, 2 * (b + 1) + hf + 1)
                    for h in range(HH):
                        mm = nc.tensor.matmul(wop_ps[hf][:, cols(h)], prob[:, cols(hf * HH + h)], wT[:, 3, :], start=True, stop=True)
                    mm.then_inc(s_wop, 1)

            def attend(at, last):
                b = num(at)
                for hf in range(2):
                    pe.wait_ge(s_wope, 2 * b + hf + 1)
                    pe.wait_ge(s_ve, 2 * b + hf + 1)
                    if not last:
                        pe.wait_ge(s_ke, 2 * (b + 1) + hf + 1)
                    for h in range(HH):
                        c = cols(hf * HH + h)
                        mm = nc.tensor.matmul(y_ps[hf][:, cols(h)], wop[:, c], vbuf[at[1]][:, c], start=True, stop=True)
                    mm.then_inc(s_att, 1)

            def att_step(at, first=False, last=False):
                scores(at)
                if not last:
                    project(nxt(at))
                if not first:
                    turn_x(prv(at), v_next=not last)
                wo_prob(at, last)
                attend(at, last)

            def turn_weights(at, m):
                n, slot, _ = mat(at, m)
                for half, (src, s_src) in enumerate(((wn_hi, s_whi), (wn_lo, s_wlo))):
                    pe.wait_ge(s_src, n + 1)
                    after(pe, s_wTe, 2 * (n - 1) + half + 1)
                    for k in range(K):
                        mm = nc.tensor.transpose(wt_ps[half][:, cols(k)], src[:, slot, cols(k)], ident16[:, :])
                    mm.then_inc(s_wT, 1)

            def gate_up(at, t, piece):
                n = TS * num(at) + t
                m, part_of = piece // 4, piece % 4
                dst = (a_ps, b_ps)[m][t % 2]
                if t == 0 and part_of == 0:
                    pe.wait_ge(s_wTe, 2 * (3 * num(at) + m) + 2)
                if piece == 0:
                    after(pe, s_h, n - 1)
                tok = slice(t * TW, (t + 1) * TW)
                hi, lo = w13_at(at[1], m, 0), w13_at(at[1], m, 1)
                for k in range(2 * part_of, 2 * part_of + 2):
                    nc.tensor.matmul(dst[:, :], hi[:, cols(k)], xT_hi[:, k, tok], start=(k == 0), stop=False)
                    nc.tensor.matmul(dst[:, :], hi[:, cols(k)], xT_lo[:, k, tok], start=False, stop=False)
                    mm = nc.tensor.matmul(dst[:, :], lo[:, cols(k)], xT_hi[:, k, tok], start=False, stop=(k == K - 1))
                if piece == 7:
                    mm.then_inc(s_ab, 1)

            def down(at, t, g):
                n = GT * num(at) + YG * t + g
                if t == 0 and g == 0:
                    pe.wait_ge(s_wTe, 2 * (3 * num(at) + 2) + 2)
                if g == 0:
                    pe.wait_ge(s_hlo, TS * num(at) + t + 1)
                after(pe, s_acc, n if t == g == 0 else n - 1)
                tok, feat = cols(t * TOK + g // 2), cols(g % 2, 512)
                dst = o_ps[g % 2]
                hi, lo = h_hi[at[1]], h_lo[at[1]]
                nc.tensor.matmul(dst[:, :], hi[:, tok], w2_at(at[1], 0)[:, feat], start=True, stop=False)
                nc.tensor.matmul(dst[:, :], hi[:, tok], w2_at(at[1], 1)[:, feat], start=False, stop=False)
                nc.tensor.matmul(dst[:, :], lo[:, tok], w2_at(at[1], 0)[:, feat], start=False, stop=True).then_inc(s_y, 1)

            def ffn_step(at, first=False, ahead=True):
                for t in range(TS):
                    for piece in range(8):
                        gate_up(at, t, piece)
                        if not first:
                            down(prv(at), t, piece)
                        if piece == 3:
                            if t == 0:
                                turn_weights(at, 2)
                            elif t < 3 and ahead:
                                turn_weights(nxt(at), t - 1)

            pe.wait_ge(s_ident, 4)
            pe.wait_ge(s_proj_in, 16 * 8)
            for n in range(4):
                nc.tensor.transpose(bank[6][:, cols(n)], w_nat[:, cols(n)], ident[:, :]).then_inc(s_projT, 1)
            pe.wait_ge(s_proj, 4)
            project((0, 0))
            att_step((0, 0), first=True)
            att_step((0, 1))
            with pe.Fori(1, B // 2 - 1) as u:
                att_step((u, 0))
                att_step((u, 1))
            att_step((B // 2 - 1, 0))
            att_step((B // 2 - 1, 1), last=True)
            turn_x((B // 2 - 1, 1), v_next=False)
            turn_weights((0, 0), 0)
            turn_weights((0, 0), 1)
            pe.wait_ge(s_xlo, 2 * B)
            ffn_step((0, 0), first=True)
            ffn_step((0, 1))
            with pe.Fori(1, NT // 2 - 1) as u:
                ffn_step((u, 0))
                ffn_step((u, 1))
            ffn_step((NT // 2 - 1, 0))
            end = ((NT - 1) // 2, 1)
            ffn_step(end, ahead=False)
            for t in range(TS):
                for g in range(YG):
                    down(end, t, g)

        @block.vector
        def _(dve):
            dve.wait_ge(s_proj_in, 16 * 8)
            nc.vector.tensor_scalar(bq_row[:, :], bq_row[:, :], SCALE, None, ALU.mult).then_inc(s_bias, 1)

            def gate():
                nc.vector.memset(gate_dve[:, :], 0.0)

            def stats(b, src, st, mv, ln, s_bn, s_mv, s_ln, scale):
                gate()
                for hf in range(2):
                    nc.vector.bn_stats(st[:, hf, :], src[:, hf * 512:(hf + 1) * 512]).then_inc(s_bn, 1)
                dve.wait_ge(s_bn, 2 * (b + 1))
                gate()
                nc.vector.bn_aggr(mv[:, :], st[:, :, :]).then_inc(s_mv, 1)
                dve.wait_ge(s_mv, b + 1)
                nc.vector.tensor_scalar(ln[:, 0:1], mv[:, 0:1], -1.0, None, ALU.mult).then_inc(s_ln, 1)
                nc.vector.tensor_scalar(ln[:, 1:2], mv[:, 1:2], EPS, scale, ALU.add, ALU.mult).then_inc(s_ln, 1)

            def x_row(b):
                return acc[:, bass.ds(b, 1), :].rearrange("p a l -> p (a l)")

            def stats_1(at):
                b = num(at)
                dve.wait_ge(x_in[at[1]], 16 * (at[0] + 1))
                after(dve, s_xn, b)
                stats(b, x_row(b), stats1, mv1, ln1, s_bn1, s_mv1, s_ln1, 1.0)

            def stats_2(at):
                b = num(at)
                dve.wait_ge(s_res, 2 * (b + 1))
                after(dve, s_x2, b)
                stats(b, x_row(b), stats2, mv2, ln2, s_bn2, s_mv2, s_ln2, 2.0 ** (-2 * XS))

            def copy_q(at, hf):
                b = num(at)
                dve.wait_ge(s_q, 2 * b + hf + 1)
                bias = bq_row[:, :].unsqueeze(1).to_broadcast([P, HH, P])
                nc.vector.scalar_tensor_tensor(out=qT[:, hf * HL:(hf + 1) * HL].rearrange("p (h o) -> p h o", h=HH),
                                               in0=q_ps[hf][:, :].rearrange("p (h o) -> p h o", h=HH), scalar=SCALE,
                                               in1=bias, op0=ALU.mult, op1=ALU.add).then_inc(s_qe, 1)

            def copy_k(at, hf):
                b = num(at)
                dve.wait_ge(s_k, 2 * b + hf + 1)
                bias = bk_row[:, :].unsqueeze(1).to_broadcast([P, HH, P])
                nc.vector.tensor_tensor(kT[:, hf * HL:(hf + 1) * HL].rearrange("p (h o) -> p h o", h=HH),
                                        k_ps[hf][:, :].rearrange("p (h o) -> p h o", h=HH), bias, ALU.add).then_inc(s_ke, 1)

            def maxes(at):
                b = num(at)
                for hf in range(2):
                    dve.wait_ge(s_score, 2 * b + hf + 1)
                    after(dve, s_exp, H * b)
                    nc.vector.tensor_reduce(nmax[:, hf * HH:(hf + 1) * HH], s_ps[hf][:, :].rearrange("p (h e) -> p h e", h=HH),
                                            AX.X, ALU.max, negate=True).then_inc(s_nmax, 1)

            def invert(at, hf):
                b = num(at)
                dve.wait_ge(s_exp, H * b + HH * (hf + 1))
                after(dve, s_prob, 2 * b)
                nc.vector.reciprocal(rinv[:, hf * HH:(hf + 1) * HH], rsum[:, hf * HH:(hf + 1) * HH]).then_inc(s_rinv, 1)

            def residual(at):
                b = num(at)
                for hf in range(2):
                    dve.wait_ge(s_att, 2 * b + hf + 1)
                    after(dve, s_xn, b + 1)
                    xs = x_row(b)[:, hf * HL:(hf + 1) * HL]
                    nc.vector.scalar_tensor_tensor(out=xs, in0=y_ps[hf][:, :], scalar=bo_col[:, 0:1], in1=xs,
                                                   op0=ALU.add, op1=ALU.add).then_inc(s_res, 1)

            def x_low(at):
                b = num(at)
                for hf in range(2):
                    dve.wait_ge(s_xhi, 2 * b + hf + 1)
                    ks = slice(hf * K // 2, (hf + 1) * K // 2)
                    nc.vector.tensor_tensor(xT_lo[:, ks, bass.ds(b * D, D)], t_ps[hf][:, :].rearrange("p (k s) -> p k s", s=D),
                                            xT_hi[:, ks, bass.ds(b * D, D)], ALU.subtract).then_inc(s_xlo, 1)

            def att_step(at, first=False, last=False, ahead=True):
                maxes(at)
                for hf in range(2):
                    if not last:
                        copy_q(nxt(at), hf)
                for hf in range(2):
                    if not last:
                        copy_k(nxt(at), hf)
                    invert(at, hf)
                if not first:
                    x_low(prv(at))
                if ahead:
                    stats_1(nxt(nxt(at)))
                residual(at)
                stats_2(at)

            def unpack(at, m):
                n, slot, nth = mat(at, m)
                i = num(at)
                dve.wait_ge(raw_in[slot], 32 * (nth + 1))
                after(dve, s_wlo, n - 1)
                if m < 2:
                    src = raw[:, slot, 0:K * G].rearrange("p (c j) -> p c j", c=K)
                    dst = q_int[:, slot, :].rearrange("p (c e j) -> p c e j", c=K, e=2)
                    high, low, high_src, low_src = dst[:, :, 0, :], dst[:, :, 1, :], src, src
                else:
                    src = raw[:, slot, :].rearrange("p (m r j) -> p m r j", m=MB, r=3)
                    dst = q_int[:, slot, :].rearrange("p (m e j) -> p m e j", m=MB, e=4)
                    high, high_src = dst[:, :, 0:4:3, :], src[:, :, 0:3:2, :]
                    low, low_src = dst[:, :, 1:3, :], src[:, :, 0:2, :]
                nc.vector.tensor_scalar(high, high_src, 4, None, ALU.arith_shift_right)
                nc.vector.tensor_scalar(low, low_src, 28, 28, ALU.logical_shift_left, ALU.arith_shift_right).then_inc(s_unp, 1)
                f = q_int[:, slot, :].bitcast(fp32)
                if m < 2:
                    q = q_int[:, slot, :].rearrange("p (g j) -> p g j", j=G)
                    w = f.rearrange("p (g j) -> p g j", j=G)
                    s = (s1_sb, s3_sb)[m][:, bass.ds(i, 1), :].rearrange("p a g -> p (a g)").unsqueeze(2).to_broadcast([P, 2 * K, G])
                else:
                    q = q_int[:, slot, :].rearrange("p (r g j) -> p r g j", r=2 * MB, j=G)
                    w = f.rearrange("p (r g j) -> p r g j", r=2 * MB, j=G)
                    s = s2_sb[:, :, bass.ds(2 * i, 2)].unsqueeze(3).to_broadcast([P, 2 * MB, 2, G])
                dve.wait_ge(s_unp, n + 1)
                nc.vector.tensor_tensor(w, q, s, ALU.mult).then_inc(s_wf, 1)

            def make_h(at, t):
                n = TS * num(at) + t
                dve.wait_ge(s_silu, n + 1)
                after(dve, s_hlo, n - 1)
                nc.vector.scalar_tensor_tensor(out=h32[t % 2], in0=b_ps[t % 2][:, :], scalar=h_scale[:, 0:1],
                                               in1=silu_sb[t % 2], op0=ALU.mult, op1=ALU.mult).then_inc(s_h, 1)

            def add_y(at, t, g):
                n = GT * num(at) + YG * t + g
                dve.wait_ge(s_y, n + 1)
                a = acc[:, t * TOK + g // 2, (g % 2) * 512:(g % 2 + 1) * 512]
                nc.vector.scalar_tensor_tensor(out=a, in0=o_ps[g % 2][:, :], scalar=y_scale[:, 0:1], in1=a,
                                               op0=ALU.mult, op1=ALU.add).then_inc(s_acc, 1)

            def ffn_step(at, first=False, ahead=True):
                for t in range(TS):
                    if ahead and t < 3:
                        unpack(nxt(at), t)
                    if not first:
                        for g in range(YG):
                            add_y(prv(at), t, g)
                    make_h(at, t)

            stats_1((0, 0))
            for hf in range(2):
                copy_q((0, 0), hf)
            for hf in range(2):
                copy_k((0, 0), hf)
            dve.wait_ge(s_scales, 16 * (4 + MB))
            for n, s_sb in enumerate((s1_sb, s3_sb, s2_sb)):
                nc.vector.tensor_reduce(smax[:, n:n + 1], s_sb[:, :, :], AX.XY, ALU.max,
                                        apply_absolute_value=True).then_inc(s_smax, 1)
            stats_1((0, 1))
            dve.wait_ge(s_smax_all, 1)
            nc.vector.tensor_scalar(smax_all[:, :], smax_all[:, :], TINY, None, ALU.max).then_inc(s_pow, 1)
            dve.wait_ge(s_pow, 1)
            nc.vector.tensor_scalar(pow2[:, :].bitcast(i32), smax_all[:, :].bitcast(i32), 0x7F800000, None,
                                    ALU.bitwise_and).then_inc(s_pow, 1)
            dve.wait_ge(s_pow, 2)
            nc.vector.reciprocal(winv[:, :], pow2[:, :]).then_inc(s_pow, 1)
            dve.wait_ge(s_pow, 3)
            nc.vector.tensor_scalar(a_scale[:, :], pow2[:, 0:1], 2.0 ** -(XS + WS), None, ALU.mult).then_inc(s_pow, 1)
            nc.vector.tensor_scalar(h_scale[:, :], winv[:, 0:1], 2.0 ** -(XS + WS + HSH), None, ALU.mult).then_inc(s_pow, 1)
            nc.vector.tensor_scalar(prod[:, :], pow2[:, 0:1], pow2[:, 1:2], 2.0 ** (HSH - WS), ALU.mult, ALU.mult).then_inc(s_pow, 1)
            dve.wait_ge(s_pow, 6)
            nc.vector.tensor_scalar(y_scale[:, :], prod[:, :], pow2[:, 2:3], None, ALU.mult).then_inc(s_pow, 1)
            nc.vector.tensor_scalar(winv[:, :], winv[:, :], 2.0 ** WS, None, ALU.mult).then_inc(s_pow, 1)
            dve.wait_ge(s_pow, 8)
            for n, s_sb in enumerate((s1_sb, s3_sb, s2_sb)):
                nc.vector.tensor_scalar(s_sb[:, :, :], s_sb[:, :, :], winv[:, n:n + 1], None, ALU.mult).then_inc(s_sc, 1)
            att_step((0, 0), first=True)
            with dve.Fori(0, B // 2 - 2) as u:
                att_step((u, 1))
                att_step((u + 1, 0))
            att_step((B // 2 - 2, 1))
            dve.wait_ge(s_sc, 3)
            unpack((0, 0), 0)
            att_step((B // 2 - 1, 0), ahead=False)
            unpack((0, 0), 1)
            att_step((B // 2 - 1, 1), last=True, ahead=False)
            x_low((B // 2 - 1, 1))
            unpack((0, 0), 2)
            ffn_step((0, 0), first=True)
            ffn_step((0, 1))
            with dve.Fori(1, NT // 2 - 1) as u:
                ffn_step((u, 0))
                ffn_step((u, 1))
            ffn_step((NT // 2 - 1, 0))
            end = ((NT - 1) // 2, 1)
            ffn_step(end, ahead=False)
            for t in range(TS):
                for g in range(YG):
                    add_y(end, t, g)


_INS = ['x', 'ctx_4096', 'L0_xattn_Wq', 'L0_xattn_bq', 'L0_xattn_Wk', 'L0_xattn_bk', 'L0_xattn_Wv', 'L0_xattn_bv',
        'L0_xattn_Wo', 'L0_xattn_bo', 'L0_ffn_w1', 'L0_ffn_s1', 'L0_ffn_w2', 'L0_ffn_s2', 'L0_ffn_w3', 'L0_ffn_s3']


def kernel(**inputs):
    import numpy as _np
    import concourse.bacc as _bacc
    from concourse import mybir as _mybir
    from concourse.bass_utils import run_bass_kernel_spmd as _run

    nc = _bacc.Bacc("TRN2", target_bir_lowering=False, num_devices=1)
    arrays, args = {}, []
    for name in _INS:
        a = _np.ascontiguousarray(inputs[name])
        arrays[f"in_{name}_dram"] = a
        args.append(nc.dram_tensor(f"in_{name}_dram", a.shape, _mybir.dt.from_np(a.dtype), kind="ExternalInput").ap())
    shape = inputs['x'].shape
    args.append(nc.dram_tensor("out_0_dram", shape, _mybir.dt.float32, kind="ExternalOutput").ap())
    bass_xattn_ffn_kernel(nc, *args)
    r = _run(nc, [arrays], core_ids=[0])
    return r.results[0]["out_0_dram"]
```

```python
import concourse.bass as bass
from concourse import mybir
from contextlib import ExitStack


def bass_xattn_ffn_kernel(nc, x, ctx_in, wq, bq, wk, bk, wv, bv, wo, bo, w1, s1, w2, s2, w3, s3, out):
    fp32, fp16, i32 = mybir.dt.float32, mybir.dt.float16, mybir.dt.int32
    ALU, ACT, AX = mybir.AluOpType, mybir.ActivationFunctionType, mybir.AxisListType

    B, D, L = x.shape
    P = 128
    H = 8
    LH = L // H
    HH = H // 2
    HL = HH * LH
    G = 64
    F = w1.shape[0] * 2 * G // L
    NT = -(-F // P)
    LAST = F - (NT - 1) * P
    K = L // P
    T = B * D
    TW = 512
    TS = T // TW
    TOK = TW // P
    YG = TOK * L // 512
    GT = TS * YG
    ROWG = F // G
    MB = L // (2 * P)
    EPS = 1e-5
    SCALE = float(LH) ** -0.5
    XS = 10
    WS = 11
    HSH = 13
    TINY = 2.0 ** -40

    with ExitStack() as stack:
        def sb(name, shape, dt):
            return stack.enter_context(nc.sbuf_tensor(name, shape, dt))

        def sem(name):
            return stack.enter_context(nc.semaphore(name))

        acc = sb("acc", [P, B, L], fp32)
        xT_hi = sb("xT_hi", [P, K, T], fp16)
        xT_lo = sb("xT_lo", [P, K, T], fp16)
        shared = sb("shared", [P, 10 * L], fp32)
        w13_even = sb("w13_even", [P, 4 * L], fp16)
        raw = sb("raw", [P, 2, 12 * G], i32)
        q_int = sb("q_int", [P, 2, L], i32)
        w_nat16 = sb("w_nat16", [P, 2, 2, L], fp16)
        s1_sb = sb("s1_sb", [P, NT, 2 * K], fp32)
        s3_sb = sb("s3_sb", [P, NT, 2 * K], fp32)
        s2_sb = sb("s2_sb", [P, 2 * MB, ROWG + 1], fp32)
        ident = sb("ident", [P, P], fp32)
        ident16 = sb("ident16", [P, P], fp16)
        wT = sb("wT", [P, 4, P], fp32)
        bq_row = sb("bq_row", [P, P], fp32)
        bk_row = sb("bk_row", [P, P], fp32)
        bv_col = sb("bv_col", [P, 1], fp32)
        bo_col = sb("bo_col", [P, 1], fp32)
        neg_half = sb("neg_half", [P, 1], fp32)
        smax = sb("smax", [P, 3], fp32)
        smax_all = sb("smax_all", [P, 3], fp32)
        pow2 = sb("pow2", [P, 3], fp32)
        winv = sb("winv", [P, 3], fp32)
        prod = sb("prod", [P, 1], fp32)
        a_scale = sb("a_scale", [P, 1], fp32)
        h_scale = sb("h_scale", [P, 1], fp32)
        y_scale = sb("y_scale", [P, 1], fp32)
        stats1 = sb("stats1", [P, 2, 6], fp32)
        stats2 = sb("stats2", [P, 2, 6], fp32)
        mv1 = sb("mv1", [P, 2], fp32)
        mv2 = sb("mv2", [P, 2], fp32)
        ln1 = sb("ln1", [P, 2], fp32)
        ln2 = sb("ln2", [P, 2], fp32)
        rstd1 = sb("rstd1", [P, 1], fp32)
        rstd2 = sb("rstd2", [P, 1], fp32)
        nb1 = sb("nb1", [P, 1], fp32)
        nb2 = sb("nb2", [P, 1], fp32)
        gate_dve = sb("gate_dve", [P, 1], fp32)
        gate_pool = sb("gate_pool", [P, 1], fp32)
        nmax = sb("nmax", [P, H], fp32)
        rsum = sb("rsum", [P, H], fp32)
        rinv = sb("rinv", [P, H], fp32)

        def part(n, count, dt=fp32):
            view = shared[:, n * L:(n + count) * L]
            return view if dt is fp32 else view.bitcast(dt)

        ctx = [part(0, 1), part(1, 1)]
        vbuf = [part(2, 1), part(3, 1)]
        xn, qT, kT, prob, wop, x2 = (part(n, 1) for n in range(4, 10))
        w_nat = part(9, 1)
        h_hi = [part(0, 1, fp16), part(1, 1, fp16)]
        h_lo = [part(2, 1, fp16), part(3, 1, fp16)]
        silu_sb = [part(4, 1)[:, 0:TW], part(4, 1)[:, TW:2 * TW]]
        h32 = [part(5, 1)[:, 0:TW], part(5, 1)[:, TW:2 * TW]]
        w13 = [w13_even[:, :], part(6, 2, fp16)]
        w2T = [part(8, 1, fp16), part(9, 1, fp16)]

        def w13_at(slot, which, half):
            o = (2 * which + half) * L
            return w13[slot][:, o:o + L]

        def w2_at(slot, half, odd):
            return w2T[slot][:, half * L:(half + 1) * L].rearrange("p (m r c) -> p r m c", m=MB, r=2)[:, odd]

        bank = [stack.enter_context(nc.psum_tensor(f"bank{n}", [P, 512], fp32)) for n in range(8)]
        q_ps, k_ps, v_ps, s_ps = bank[0:2], bank[2:4], bank[4:6], bank[6:8]
        wop_ps, y_ps, t_ps = bank[0:2], bank[2:4], bank[4:6]
        a_ps, b_ps, o_ps = [bank[0], bank[2]], [bank[1], bank[3]], [bank[4], bank[5]]

        s_zero = sem("s_zero")
        s_scales = sem("s_scales")
        s_proj_in = sem("s_proj_in")
        s_ident = sem("s_ident")
        s_projT = sem("s_projT")
        s_proj = sem("s_proj")
        s_bias = sem("s_bias")
        s_smax = sem("s_smax")
        s_smax_all = sem("s_smax_all")
        s_pow = sem("s_pow")
        s_sc = sem("s_sc")
        x_in = [sem("x_in0"), sem("x_in1")]
        c_in = [sem("c_in0"), sem("c_in1")]
        s_bn1, s_mv1, s_ln1, s_rstd1, s_xn = (sem(n) for n in ("s_bn1", "s_mv1", "s_ln1", "s_rstd1", "s_xn"))
        s_bn2, s_mv2, s_ln2, s_rstd2, s_x2 = (sem(n) for n in ("s_bn2", "s_mv2", "s_ln2", "s_rstd2", "s_x2"))
        s_nb1, s_nb2 = sem("s_nb1"), sem("s_nb2")
        s_q, s_k, s_v = sem("s_q"), sem("s_k"), sem("s_v")
        s_qe, s_ke, s_ve = sem("s_qe"), sem("s_ke"), sem("s_ve")
        s_score = sem("s_score")
        s_nmax = sem("s_nmax")
        s_exp = sem("s_exp")
        s_rinv = sem("s_rinv")
        s_prob = sem("s_prob")
        s_wop = sem("s_wop")
        s_wope = sem("s_wope")
        s_att = sem("s_att")
        s_res = sem("s_res")
        s_xT = sem("s_xT")
        s_xhi, s_xlo = sem("s_xhi"), sem("s_xlo")
        raw_in = [sem("raw_in0"), sem("raw_in1")]
        s_unp = sem("s_unp")
        s_wf, s_whi, s_wlo = sem("s_wf"), sem("s_whi"), sem("s_wlo")
        s_turn = sem("s_turn")
        w_in = [sem("w1_in"), sem("w3_in"), sem("w2_in")]
        s_ab = sem("s_ab")
        s_silu, s_h, s_hhi, s_hlo = sem("s_silu"), sem("s_h"), sem("s_hhi"), sem("s_hlo")
        s_y = sem("s_y")
        s_acc = sem("s_acc")
        s_out = sem("s_out")

        def after(eng, s, count):
            if not (type(count) is int and count <= 0):
                eng.wait_ge(s, count)

        def num(at):
            return 2 * at[0] + at[1]

        def nxt(at):
            return (at[0], 1) if at[1] == 0 else (at[0] + 1, 0)

        def prv(at):
            return (at[0], 0) if at[1] == 1 else (at[0] - 1, 1)

        def mat(at, m):
            return 3 * num(at) + m, (3 * at[1] + m) % 2, 3 * at[0] + (3 * at[1] + m) // 2

        w1_rows = w1.rearrange("(h c) j -> h c j", c=K)
        w3_rows = w3.rearrange("(h c) j -> h c j", c=K)
        w2_rows = w2.rearrange("(m p r) j -> p m r j", p=P, r=ROWG)

        tiles = range(NT)
        block = stack.enter_context(nc.Block())

        @block.sync
        def _(sp):
            with nc.allow_non_contiguous_dma(reason="biases, one value per partition, once"):
                for n, w in enumerate((wq, wk, wv, wo)):
                    sp.dma_start(w_nat[:, n * P:(n + 1) * P], w).then_inc(s_proj_in, 16)
                sp.dma_start(bq_row[:, :], bq.rearrange("(a o) -> a o", a=1).to_broadcast([P, P])).then_inc(s_proj_in, 16)
                sp.dma_start(bk_row[:, :], bk.rearrange("(a o) -> a o", a=1).to_broadcast([P, P])).then_inc(s_proj_in, 16)
                sp.dma_start(bv_col[:, :], bv.rearrange("(o a) -> o a", a=1)).then_inc(s_proj_in, 16)
                sp.dma_start(bo_col[:, :], bo.rearrange("(o a) -> o a", a=1)).then_inc(s_proj_in, 16)

            def load_batch(at):
                b = num(at)
                after(sp, s_mv1, b - 1)
                sp.dma_start(acc[:, bass.ds(b, 1), :], x[bass.ds(b, 1)].rearrange("b s l -> s b l")).then_inc(x_in[at[1]], 16)
                after(sp, s_v, 2 * (b - 1))
                sp.dma_start(ctx[at[1]], ctx_in[bass.ds(b, 1)].rearrange("b s l -> s (b l)")).then_inc(c_in[at[1]], 16)

            load_batch((0, 0))
            load_batch((0, 1))

            sp.wait_ge(s_zero, 3)
            full = (NT - 1) * P
            with nc.allow_non_contiguous_dma(reason="scales, once"):
                for s, s_sb in ((s1, s1_sb), (s3, s3_sb)):
                    rows = s.rearrange("(h g) -> h g", g=2 * K)
                    sp.dma_start(s_sb[:, 0:NT - 1, :], rows[0:full].rearrange("(i p) g -> p i g", p=P)).then_inc(s_scales, 16)
                    sp.dma_start(s_sb[0:LAST, NT - 1, :], rows[full:F]).then_inc(s_scales, 16)
                pairs = s2.rearrange("(m p r k) -> m p r k", p=P, r=2, k=ROWG)
                for m in range(MB):
                    sp.dma_start(s2_sb[:, 2 * m:2 * m + 2, 0:ROWG], pairs[m]).then_inc(s_scales, 16)

            def load_weights(at, m):
                n, slot, _ = mat(at, m)
                i = num(at)
                dst = raw[:, slot, :]
                after(sp, s_unp, n - 1)
                if m < 2:
                    src = w1_rows if m == 0 else w3_rows
                    d = dst[:, 0:K * G].rearrange("p (c j) -> p c j", c=K)
                    half = K // 2
                    if type(i) is int and i == NT - 1:
                        for c in (0, half):
                            sp.dma_start(d[0:LAST, c:c + half, :], src[i * P:F, c:c + half, :]).then_inc(raw_in[slot], 16)
                    else:
                        for c in (0, half):
                            sp.dma_start(d[:, c:c + half, :], src[bass.ds(i * P, P), c:c + half, :]).then_inc(raw_in[slot], 16)
                else:
                    d = dst.rearrange("p (m r j) -> p m r j", m=MB, r=3)
                    first = ROWG // 2 + i
                    sp.dma_start(d[:, :, 0:1, :], w2_rows[:, :, bass.ds(i, 1), :]).then_inc(raw_in[slot], 16)
                    if type(i) is int and i == NT - 1:
                        sp.dma_start(d[:, :, 1:2, :], w2_rows[:, :, first:first + 1, :]).then_inc(raw_in[slot], 16)
                    else:
                        sp.dma_start(d[:, :, 1:3, :], w2_rows[:, :, bass.ds(first, 2), :]).then_inc(raw_in[slot], 16)

            load_weights((0, 0), 0)
            load_weights((0, 0), 1)
            with sp.Fori(1, B // 2) as u:
                load_batch((u, 0))
                load_batch((u, 1))
            load_weights((0, 0), 2)
            with sp.Fori(0, (NT - 2) // 2) as u:
                for at in ((u, 1), (u + 1, 0)):
                    for m in range(3):
                        load_weights(at, m)
            for m in range(3):
                load_weights(((NT - 1) // 2, 1), m)

            with sp.Fori(0, B) as b:
                sp.wait_ge(s_acc, GT * (NT - 1) + 2 * (b + 1))
                sp.dma_start(out[bass.ds(b, 1)].rearrange("b s l -> s b l"), acc[:, bass.ds(b, 1), :]).then_inc(s_out, 16)
            sp.wait_ge(s_out, 16 * B)

        @block.gpsimd
        def _(pool):
            nc.gpsimd.memset(s1_sb[:, :, :], 0.0).then_inc(s_zero, 1)
            nc.gpsimd.memset(s3_sb[:, :, :], 0.0).then_inc(s_zero, 1)
            nc.gpsimd.memset(s2_sb[:, :, :], 0.0).then_inc(s_zero, 1)
            nc.gpsimd.memset(neg_half[:, :], -0.5)
            nc.gpsimd.memset(ident16[:, :], 0.0).then_inc(s_ident, 1)
            nc.gpsimd.memset(ident[:, :], 0.0).then_inc(s_ident, 1)
            pool.wait_ge(s_ident, 2)
            for m in (ident, ident16):
                nc.gpsimd.affine_select(out=m[:, :], in_=m[:, :], compare_op=ALU.not_equal, fill=1.0, base=0,
                                        pattern=[[-1, P]], channel_multiplier=1).then_inc(s_ident, 1)

            def gate():
                nc.gpsimd.tensor_tensor(gate_pool[:, :], neg_half[:, :], neg_half[:, :], ALU.add)

            def rstd(b, s_ln, ln, s_rstd, r, s_nb, nb, s_used):
                pool.wait_ge(s_ln, 2 * (b + 1))
                after(pool, s_used, b)
                nc.gpsimd.tensor_tensor(r[:, :], ln[:, 1:2], neg_half[:, :], ALU.pow).then_inc(s_rstd, 1)
                pool.wait_ge(s_rstd, b + 1)
                nc.gpsimd.tensor_tensor(nb[:, :], ln[:, 0:1], r[:, :], ALU.mult).then_inc(s_nb, 1)

            def rstd_1(at):
                rstd(num(at), s_ln1, ln1, s_rstd1, rstd1, s_nb1, nb1, s_xn)

            def rstd_2(at):
                rstd(num(at), s_ln2, ln2, s_rstd2, rstd2, s_nb2, nb2, s_x2)

            def scale_prob(at):
                b = num(at)
                for hf in range(2):
                    pool.wait_ge(s_rinv, 2 * b + hf + 1)
                    p = prob[:, hf * HL:(hf + 1) * HL].rearrange("p (h e) -> p h e", h=HH)
                    r = rinv[:, hf * HH:(hf + 1) * HH].unsqueeze(2).to_broadcast([P, HH, LH])
                    nc.gpsimd.tensor_tensor(p, p, r, ALU.mult).then_inc(s_prob, 1)

            def att_step(at, first=False, ahead=True):
                if not first:
                    rstd_2(prv(at))
                scale_prob(at)
                if ahead:
                    rstd_1(nxt(nxt(at)))

            def split(at, m):
                n, slot, _ = mat(at, m)
                f = q_int[:, slot, :].bitcast(fp32)
                pool.wait_ge(s_wf, n + 1)
                before = (m + 1) % 3
                after(pool, w_in[before], 16 * (num(at) + 1 if m == 2 else num(at)))
                gate()
                nc.gpsimd.tensor_scalar(w_nat16[:, slot, 0, :], f, 1.0, 1.0, ALU.mult, ALU.mult).then_inc(s_whi, 1)
                pool.wait_ge(s_whi, n + 1)
                nc.gpsimd.tensor_tensor(w_nat16[:, slot, 1, :], f, w_nat16[:, slot, 0, :], ALU.subtract).then_inc(s_wlo, 1)

            def h_low(at, t):
                n = TS * num(at) + t
                o = t * TW
                pool.wait_ge(s_hhi, n + 1)
                nc.gpsimd.tensor_tensor(h_lo[at[1]][:, o:o + TW], h32[t % 2], h_hi[at[1]][:, o:o + TW],
                                        ALU.subtract).then_inc(s_hlo, 1)

            def ffn_step(at, ahead=True):
                for t in range(TS):
                    if ahead and t < 3:
                        split(nxt(at), t)
                    h_low(at, t)

            rstd_1((0, 0))
            pool.wait_ge(s_smax, 3)
            nc.gpsimd.partition_all_reduce(smax_all[:, :], smax[:, :], P, bass.bass_isa.ReduceOp.max).then_inc(s_smax_all, 1)
            rstd_1((0, 1))
            att_step((0, 0), first=True)
            att_step((0, 1))
            with pool.Fori(1, B // 2 - 1) as u:
                att_step((u, 0))
                att_step((u, 1))
            split((0, 0), 0)
            att_step((B // 2 - 1, 0), ahead=False)
            split((0, 0), 1)
            att_step((B // 2 - 1, 1), ahead=False)
            rstd_2((B // 2 - 1, 1))
            split((0, 0), 2)
            ffn_step((0, 0))
            ffn_step((0, 1))
            with pool.Fori(1, NT // 2 - 1) as u:
                ffn_step((u, 0))
                ffn_step((u, 1))
            ffn_step((NT // 2 - 1, 0))
            ffn_step(((NT - 1) // 2, 1), ahead=False)

        @block.scalar
        def _(act):
            def copy_v(at):
                b = num(at)
                for hf in range(2):
                    act.wait_ge(s_v, 2 * b + hf + 1)
                    after(act, s_att, 2 * (b - 1))
                    nc.scalar.activation(vbuf[at[1]][:, hf * HL:(hf + 1) * HL], v_ps[hf][:, :], ACT.Identity,
                                         bias=bv_col[:, 0:1]).then_inc(s_ve, 1)

            def exps(at):
                b = num(at)
                for h in range(H):
                    hf, o = h // HH, (h % HH) * LH
                    if h % HH == 0:
                        act.wait_ge(s_nmax, 2 * b + hf + 1)
                        after(act, s_wop, 2 * b)
                        after(act, s_rinv, 2 * b)
                    nc.scalar.activation(prob[:, h * LH:(h + 1) * LH], s_ps[hf][:, o:o + LH], ACT.Exp,
                                         bias=nmax[:, h:h + 1], accum_out=rsum[:, h:h + 1]).then_inc(s_exp, 1)

            def copy_wop(at):
                b = num(at)
                for hf in range(2):
                    act.wait_ge(s_wop, 2 * b + hf + 1)
                    after(act, s_att, 2 * b)
                    nc.scalar.activation(wop[:, hf * HL:(hf + 1) * HL], wop_ps[hf][:, :], ACT.Copy).then_inc(s_wope, 1)

            def x_high(at):
                b = num(at)
                for hf in range(2):
                    act.wait_ge(s_xT, 2 * b + hf + 1)
                    nc.scalar.activation(xT_hi[:, hf * K // 2:(hf + 1) * K // 2, bass.ds(b * D, D)],
                                         t_ps[hf][:, :].rearrange("p (k s) -> p k s", s=D), ACT.Copy).then_inc(s_xhi, 1)

            def norm(b, s_nb, nb, r, dst, s_free, s_done):
                after(act, s_free, 2 * b)
                act.wait_ge(s_nb, b + 1)
                nc.scalar.activation(dst, acc[:, bass.ds(b, 1), :].rearrange("p a l -> p (a l)"), ACT.Identity,
                                     bias=nb[:, 0:1], scale=r[:, 0:1]).then_inc(s_done, 1)

            def norm_1(at):
                norm(num(at), s_nb1, nb1, rstd1, xn, s_q, s_xn)

            def norm_2(at):
                norm(num(at), s_nb2, nb2, rstd2, x2, s_xT, s_x2)

            def att_step(at, first=False, last=False, ahead=True):
                exps(at)
                if not first:
                    norm_2(prv(at))
                if not last:
                    copy_v(nxt(at))
                if not first:
                    x_high(prv(at))
                copy_wop(at)
                if ahead:
                    norm_1(nxt(nxt(at)))

            def weight_slot(at, m):
                n, slot, _ = mat(at, m)
                i = num(at)
                if m < 2:
                    after(act, s_ab, TS * (i - 1))
                    dst = w13[at[1]][:, 2 * m * L:2 * (m + 1) * L]
                else:
                    after(act, s_y, GT * (i - 1))
                    dst = w2T[at[1]]
                act.wait_ge(s_wlo, n + 1)
                nc.scalar.sem_inc(s_turn, 1)
                act.dma_start(dst.rearrange("p (c r) -> p c r", r=P), w_nat16[:, slot, :, :].rearrange("p h l -> p (h l)"),
                              transpose=True).then_inc(w_in[m], 16)

            def ffn_step(at, ahead=True):
                for t in range(TS):
                    n = TS * num(at) + t
                    act.wait_ge(s_ab, n + 1)
                    nc.scalar.activation(silu_sb[t % 2], a_ps[t % 2][:, :], ACT.Silu, scale=a_scale[:, 0:1]).then_inc(s_silu, 1)
                    if t == 0:
                        weight_slot(at, 2)
                    elif t < 3 and ahead:
                        weight_slot(nxt(at), t - 1)
                    act.wait_ge(s_h, n + 1)
                    after(act, s_y, GT * (num(at) - 1))
                    nc.scalar.activation(h_hi[at[1]][:, t * TW:(t + 1) * TW], h32[t % 2], ACT.Copy).then_inc(s_hhi, 1)

            act.wait_ge(s_projT, 4)
            for n in range(4):
                nc.scalar.activation(wT[:, n, :], bank[6][:, n * P:(n + 1) * P], ACT.Copy).then_inc(s_proj, 1)
            act.wait_ge(s_proj_in, 16 * 8)
            norm_1((0, 0))
            copy_v((0, 0))
            norm_1((0, 1))
            att_step((0, 0), first=True)
            att_step((0, 1))
            with act.Fori(1, B // 2 - 1) as u:
                att_step((u, 0))
                att_step((u, 1))
            att_step((B // 2 - 1, 0), ahead=False)
            att_step((B // 2 - 1, 1), last=True, ahead=False)
            norm_2((B // 2 - 1, 1))
            x_high((B // 2 - 1, 1))
            weight_slot((0, 0), 0)
            weight_slot((0, 0), 1)
            act.wait_ge(s_pow, 8)
            ffn_step((0, 0))
            ffn_step((0, 1))
            with act.Fori(1, NT // 2 - 1) as u:
                ffn_step((u, 0))
                ffn_step((u, 1))
            ffn_step((NT // 2 - 1, 0))
            ffn_step(((NT - 1) // 2, 1), ahead=False)

        @block.tensor
        def _(pe):
            def cols(n, w=P):
                return slice(n * w, (n + 1) * w)

            def project(at):
                b = num(at)
                pe.wait_ge(s_xn, b + 1)
                pe.wait_ge(c_in[at[1]], 16 * (at[0] + 1))
                for hf in range(2):
                    after(pe, s_wope, 2 * (b - 2) + hf + 1)
                    for h in range(HH):
                        mm = nc.tensor.matmul(q_ps[hf][:, cols(h)], xn[:, cols(hf * HH + h)], wT[:, 0, :], start=True, stop=True)
                    mm.then_inc(s_q, 1)
                for hf in range(2):
                    after(pe, s_res, 2 * (b - 2) + hf + 1)
                    for h in range(HH):
                        mm = nc.tensor.matmul(k_ps[hf][:, cols(h)], ctx[at[1]][:, cols(hf * HH + h)], wT[:, 1, :], start=True, stop=True)
                    mm.then_inc(s_k, 1)
                for hf in range(2):
                    after(pe, s_ve, 2 * (b - 1) + hf + 1)
                    after(pe, s_xlo, 2 * (b - 3) + hf + 1)
                    nc.tensor.matmul(v_ps[hf][:, :], wT[:, 2, :], ctx[at[1]][:, cols(hf, HL)], start=True, stop=True).then_inc(s_v, 1)

            def scores(at):
                b = num(at)
                for hf in range(2):
                    pe.wait_ge(s_qe, 2 * b + hf + 1)
                    pe.wait_ge(s_ke, 2 * b + hf + 1)
                    after(pe, s_exp, H * (b - 1) + HH * (hf + 1))
                    for h in range(HH):
                        c = cols(hf * HH + h)
                        mm = nc.tensor.matmul(s_ps[hf][:, cols(h)], qT[:, c], kT[:, c], start=True, stop=True)
                    mm.then_inc(s_score, 1)

            def turn_x(at, v_next):
                b = num(at)
                pe.wait_ge(s_x2, b + 1)
                for hf in range(2):
                    if v_next:
                        pe.wait_ge(s_ve, 2 * (b + 2) + hf + 1)
                    else:
                        after(pe, s_xlo, 2 * (b - 1) + hf + 1)
                    for k in range(K // 2):
                        mm = nc.tensor.transpose(t_ps[hf][:, cols(k)], x2[:, cols(hf * K // 2 + k)], ident[:, :])
                    mm.then_inc(s_xT, 1)

            def wo_prob(at, last):
                b = num(at)
                for hf in range(2):
                    pe.wait_ge(s_prob, 2 * b + hf + 1)
                    if not last:
                        pe.wait_ge(s_qe, 2 * (b + 1) + hf + 1)
                    for h in range(HH):
                        mm = nc.tensor.matmul(wop_ps[hf][:, cols(h)], prob[:, cols(hf * HH + h)], wT[:, 3, :], start=True, stop=True)
                    mm.then_inc(s_wop, 1)

            def attend(at, last):
                b = num(at)
                for hf in range(2):
                    pe.wait_ge(s_wope, 2 * b + hf + 1)
                    pe.wait_ge(s_ve, 2 * b + hf + 1)
                    if not last:
                        pe.wait_ge(s_ke, 2 * (b + 1) + hf + 1)
                    for h in range(HH):
                        c = cols(hf * HH + h)
                        mm = nc.tensor.matmul(y_ps[hf][:, cols(h)], wop[:, c], vbuf[at[1]][:, c], start=True, stop=True)
                    mm.then_inc(s_att, 1)

            def att_step(at, first=False, last=False):
                scores(at)
                if not last:
                    project(nxt(at))
                if not first:
                    turn_x(prv(at), v_next=not last)
                wo_prob(at, last)
                attend(at, last)

            def gate_up(at, t, piece):
                n = TS * num(at) + t
                m, part_of = piece // 4, piece % 4
                dst = (a_ps, b_ps)[m][t % 2]
                if t == 0 and part_of == 0:
                    pe.wait_ge(w_in[m], 16 * (num(at) + 1))
                if piece == 0:
                    after(pe, s_h, n - 1)
                tok = slice(t * TW, (t + 1) * TW)
                hi, lo = w13_at(at[1], m, 0), w13_at(at[1], m, 1)
                for k in range(2 * part_of, 2 * part_of + 2):
                    nc.tensor.matmul(dst[:, :], hi[:, cols(k)], xT_hi[:, k, tok], start=(k == 0), stop=False)
                    nc.tensor.matmul(dst[:, :], hi[:, cols(k)], xT_lo[:, k, tok], start=False, stop=False)
                    mm = nc.tensor.matmul(dst[:, :], lo[:, cols(k)], xT_hi[:, k, tok], start=False, stop=(k == K - 1))
                if piece == 7:
                    mm.then_inc(s_ab, 1)

            def down(at, t, g):
                n = GT * num(at) + YG * t + g
                if t == 0 and g == 0:
                    pe.wait_ge(w_in[2], 16 * (num(at) + 1))
                if g == 0:
                    pe.wait_ge(s_hlo, TS * num(at) + t + 1)
                after(pe, s_acc, n if t == g == 0 else n - 1)
                tok, odd = cols(t * TOK + g // 2), g % 2
                dst = o_ps[g % 2][:, :].rearrange("p (m c) -> p m c", m=MB)
                hi, lo = h_hi[at[1]], h_lo[at[1]]
                nc.tensor.matmul(dst, hi[:, tok], w2_at(at[1], 0, odd), start=True, stop=False)
                nc.tensor.matmul(dst, hi[:, tok], w2_at(at[1], 1, odd), start=False, stop=False)
                nc.tensor.matmul(dst, lo[:, tok], w2_at(at[1], 0, odd), start=False, stop=True).then_inc(s_y, 1)

            def ffn_step(at, first=False):
                for t in range(TS):
                    for piece in range(8):
                        gate_up(at, t, piece)
                        if not first:
                            down(prv(at), t, piece)

            pe.wait_ge(s_ident, 4)
            pe.wait_ge(s_proj_in, 16 * 8)
            for n in range(4):
                nc.tensor.transpose(bank[6][:, cols(n)], w_nat[:, cols(n)], ident[:, :]).then_inc(s_projT, 1)
            pe.wait_ge(s_proj, 4)
            project((0, 0))
            att_step((0, 0), first=True)
            att_step((0, 1))
            with pe.Fori(1, B // 2 - 1) as u:
                att_step((u, 0))
                att_step((u, 1))
            att_step((B // 2 - 1, 0))
            att_step((B // 2 - 1, 1), last=True)
            turn_x((B // 2 - 1, 1), v_next=False)
            pe.wait_ge(s_xlo, 2 * B)
            ffn_step((0, 0), first=True)
            ffn_step((0, 1))
            with pe.Fori(1, NT // 2 - 1) as u:
                ffn_step((u, 0))
                ffn_step((u, 1))
            ffn_step((NT // 2 - 1, 0))
            end = ((NT - 1) // 2, 1)
            ffn_step(end)
            for t in range(TS):
                for g in range(YG):
                    down(end, t, g)

        @block.vector
        def _(dve):
            dve.wait_ge(s_proj_in, 16 * 8)
            nc.vector.tensor_scalar(bq_row[:, :], bq_row[:, :], SCALE, None, ALU.mult).then_inc(s_bias, 1)

            def gate():
                nc.vector.memset(gate_dve[:, :], 0.0)

            def stats(b, src, st, mv, ln, s_bn, s_mv, s_ln, scale):
                gate()
                for hf in range(2):
                    nc.vector.bn_stats(st[:, hf, :], src[:, hf * 512:(hf + 1) * 512]).then_inc(s_bn, 1)
                dve.wait_ge(s_bn, 2 * (b + 1))
                gate()
                nc.vector.bn_aggr(mv[:, :], st[:, :, :]).then_inc(s_mv, 1)
                dve.wait_ge(s_mv, b + 1)
                nc.vector.tensor_scalar(ln[:, 0:1], mv[:, 0:1], -1.0, None, ALU.mult).then_inc(s_ln, 1)
                nc.vector.tensor_scalar(ln[:, 1:2], mv[:, 1:2], EPS, scale, ALU.add, ALU.mult).then_inc(s_ln, 1)

            def x_row(b):
                return acc[:, bass.ds(b, 1), :].rearrange("p a l -> p (a l)")

            def stats_1(at):
                b = num(at)
                dve.wait_ge(x_in[at[1]], 16 * (at[0] + 1))
                after(dve, s_nb1, b)
                stats(b, x_row(b), stats1, mv1, ln1, s_bn1, s_mv1, s_ln1, 1.0)

            def stats_2(at):
                b = num(at)
                dve.wait_ge(s_res, 2 * (b + 1))
                after(dve, s_nb2, b)
                stats(b, x_row(b), stats2, mv2, ln2, s_bn2, s_mv2, s_ln2, 2.0 ** (-2 * XS))

            def copy_q(at, hf):
                b = num(at)
                dve.wait_ge(s_q, 2 * b + hf + 1)
                bias = bq_row[:, :].unsqueeze(1).to_broadcast([P, HH, P])
                nc.vector.scalar_tensor_tensor(out=qT[:, hf * HL:(hf + 1) * HL].rearrange("p (h o) -> p h o", h=HH),
                                               in0=q_ps[hf][:, :].rearrange("p (h o) -> p h o", h=HH), scalar=SCALE,
                                               in1=bias, op0=ALU.mult, op1=ALU.add).then_inc(s_qe, 1)

            def copy_k(at, hf):
                b = num(at)
                dve.wait_ge(s_k, 2 * b + hf + 1)
                bias = bk_row[:, :].unsqueeze(1).to_broadcast([P, HH, P])
                nc.vector.tensor_tensor(kT[:, hf * HL:(hf + 1) * HL].rearrange("p (h o) -> p h o", h=HH),
                                        k_ps[hf][:, :].rearrange("p (h o) -> p h o", h=HH), bias, ALU.add).then_inc(s_ke, 1)

            def maxes(at):
                b = num(at)
                for hf in range(2):
                    dve.wait_ge(s_score, 2 * b + hf + 1)
                    after(dve, s_exp, H * b)
                    nc.vector.tensor_reduce(nmax[:, hf * HH:(hf + 1) * HH], s_ps[hf][:, :].rearrange("p (h e) -> p h e", h=HH),
                                            AX.X, ALU.max, negate=True).then_inc(s_nmax, 1)

            def invert(at, hf):
                b = num(at)
                dve.wait_ge(s_exp, H * b + HH * (hf + 1))
                after(dve, s_prob, 2 * b)
                nc.vector.reciprocal(rinv[:, hf * HH:(hf + 1) * HH], rsum[:, hf * HH:(hf + 1) * HH]).then_inc(s_rinv, 1)

            def residual(at):
                b = num(at)
                for hf in range(2):
                    dve.wait_ge(s_att, 2 * b + hf + 1)
                    after(dve, s_xn, b + 1)
                    xs = x_row(b)[:, hf * HL:(hf + 1) * HL]
                    nc.vector.scalar_tensor_tensor(out=xs, in0=y_ps[hf][:, :], scalar=bo_col[:, 0:1], in1=xs,
                                                   op0=ALU.add, op1=ALU.add).then_inc(s_res, 1)

            def x_low(at):
                b = num(at)
                for hf in range(2):
                    dve.wait_ge(s_xhi, 2 * b + hf + 1)
                    ks = slice(hf * K // 2, (hf + 1) * K // 2)
                    nc.vector.tensor_tensor(xT_lo[:, ks, bass.ds(b * D, D)], t_ps[hf][:, :].rearrange("p (k s) -> p k s", s=D),
                                            xT_hi[:, ks, bass.ds(b * D, D)], ALU.subtract).then_inc(s_xlo, 1)

            def att_step(at, first=False, last=False, ahead=True):
                maxes(at)
                if not first:
                    stats_2(prv(at))
                for hf in range(2):
                    invert(at, hf)
                    if not last:
                        copy_q(nxt(at), hf)
                for hf in range(2):
                    if not last:
                        copy_k(nxt(at), hf)
                if ahead:
                    stats_1(nxt(nxt(at)))
                if not first:
                    x_low(prv(at))
                residual(at)

            def unpack(at, m):
                n, slot, nth = mat(at, m)
                i = num(at)
                dve.wait_ge(raw_in[slot], 32 * (nth + 1))
                after(dve, s_wlo, n - 1)
                if m < 2:
                    src = raw[:, slot, 0:K * G].rearrange("p (c j) -> p c j", c=K)
                    dst = q_int[:, slot, :].rearrange("p (c e j) -> p c e j", c=K, e=2)
                    high, low, high_src, low_src = dst[:, :, 0, :], dst[:, :, 1, :], src, src
                else:
                    src = raw[:, slot, :].rearrange("p (m r j) -> p m r j", m=MB, r=3)
                    dst = q_int[:, slot, :].rearrange("p (m e j) -> p m e j", m=MB, e=4)
                    high, high_src = dst[:, :, 0:4:3, :], src[:, :, 0:3:2, :]
                    low, low_src = dst[:, :, 1:3, :], src[:, :, 0:2, :]
                nc.vector.tensor_scalar(high, high_src, 4, None, ALU.arith_shift_right)
                nc.vector.tensor_scalar(low, low_src, 28, 28, ALU.logical_shift_left, ALU.arith_shift_right).then_inc(s_unp, 1)
                f = q_int[:, slot, :].bitcast(fp32)
                if m < 2:
                    q = q_int[:, slot, :].rearrange("p (g j) -> p g j", j=G)
                    w = f.rearrange("p (g j) -> p g j", j=G)
                    s = (s1_sb, s3_sb)[m][:, bass.ds(i, 1), :].rearrange("p a g -> p (a g)").unsqueeze(2).to_broadcast([P, 2 * K, G])
                else:
                    q = q_int[:, slot, :].rearrange("p (r g j) -> p r g j", r=2 * MB, j=G)
                    w = f.rearrange("p (r g j) -> p r g j", r=2 * MB, j=G)
                    s = s2_sb[:, :, bass.ds(2 * i, 2)].unsqueeze(3).to_broadcast([P, 2 * MB, 2, G])
                dve.wait_ge(s_unp, n + 1)
                nc.vector.tensor_tensor(w, q, s, ALU.mult).then_inc(s_wf, 1)

            def make_h(at, t):
                n = TS * num(at) + t
                dve.wait_ge(s_silu, n + 1)
                after(dve, s_hlo, n - 1)
                nc.vector.scalar_tensor_tensor(out=h32[t % 2], in0=b_ps[t % 2][:, :], scalar=h_scale[:, 0:1],
                                               in1=silu_sb[t % 2], op0=ALU.mult, op1=ALU.mult).then_inc(s_h, 1)

            def add_y(at, t, g):
                n = GT * num(at) + YG * t + g
                dve.wait_ge(s_y, n + 1)
                a = acc[:, t * TOK + g // 2, :].rearrange("p (m c r) -> p r m c", m=MB, r=2)[:, g % 2]
                y = o_ps[g % 2][:, :].rearrange("p (m c) -> p m c", m=MB)
                nc.vector.scalar_tensor_tensor(out=a, in0=y, scalar=y_scale[:, 0:1], in1=a,
                                               op0=ALU.mult, op1=ALU.add).then_inc(s_acc, 1)

            def ffn_step(at, first=False, ahead=True):
                for t in range(TS):
                    if ahead and t < 3:
                        unpack(nxt(at), t)
                    if not first:
                        for g in range(YG):
                            add_y(prv(at), t, g)
                    make_h(at, t)

            stats_1((0, 0))
            for hf in range(2):
                copy_q((0, 0), hf)
            for hf in range(2):
                copy_k((0, 0), hf)
            dve.wait_ge(s_scales, 16 * (4 + MB))
            for n, s_sb in enumerate((s1_sb, s3_sb, s2_sb)):
                nc.vector.tensor_reduce(smax[:, n:n + 1], s_sb[:, :, :], AX.XY, ALU.max,
                                        apply_absolute_value=True).then_inc(s_smax, 1)
            stats_1((0, 1))
            dve.wait_ge(s_smax_all, 1)
            nc.vector.tensor_scalar(smax_all[:, :], smax_all[:, :], TINY, None, ALU.max).then_inc(s_pow, 1)
            dve.wait_ge(s_pow, 1)
            nc.vector.tensor_scalar(pow2[:, :].bitcast(i32), smax_all[:, :].bitcast(i32), 0x7F800000, None,
                                    ALU.bitwise_and).then_inc(s_pow, 1)
            dve.wait_ge(s_pow, 2)
            nc.vector.reciprocal(winv[:, :], pow2[:, :]).then_inc(s_pow, 1)
            dve.wait_ge(s_pow, 3)
            nc.vector.tensor_scalar(a_scale[:, :], pow2[:, 0:1], 2.0 ** -(XS + WS), None, ALU.mult).then_inc(s_pow, 1)
            nc.vector.tensor_scalar(h_scale[:, :], winv[:, 0:1], 2.0 ** -(XS + WS + HSH), None, ALU.mult).then_inc(s_pow, 1)
            nc.vector.tensor_scalar(prod[:, :], pow2[:, 0:1], pow2[:, 1:2], 2.0 ** (HSH - WS), ALU.mult, ALU.mult).then_inc(s_pow, 1)
            dve.wait_ge(s_pow, 6)
            nc.vector.tensor_scalar(y_scale[:, :], prod[:, :], pow2[:, 2:3], None, ALU.mult).then_inc(s_pow, 1)
            nc.vector.tensor_scalar(winv[:, :], winv[:, :], 2.0 ** WS, None, ALU.mult).then_inc(s_pow, 1)
            dve.wait_ge(s_pow, 8)
            for n, s_sb in enumerate((s1_sb, s3_sb, s2_sb)):
                nc.vector.tensor_scalar(s_sb[:, :, :], s_sb[:, :, :], winv[:, n:n + 1], None, ALU.mult).then_inc(s_sc, 1)
            att_step((0, 0), first=True)
            att_step((0, 1))
            with dve.Fori(1, B // 2 - 1) as u:
                att_step((u, 0))
                att_step((u, 1))
            dve.wait_ge(s_sc, 3)
            unpack((0, 0), 0)
            att_step((B // 2 - 1, 0), ahead=False)
            unpack((0, 0), 1)
            att_step((B // 2 - 1, 1), last=True, ahead=False)
            stats_2((B // 2 - 1, 1))
            x_low((B // 2 - 1, 1))
            unpack((0, 0), 2)
            ffn_step((0, 0), first=True)
            ffn_step((0, 1))
            with dve.Fori(1, NT // 2 - 1) as u:
                ffn_step((u, 0))
                ffn_step((u, 1))
            ffn_step((NT // 2 - 1, 0))
            end = ((NT - 1) // 2, 1)
            ffn_step(end, ahead=False)
            for t in range(TS):
                for g in range(YG):
                    add_y(end, t, g)


_INS = ['x', 'ctx_4096', 'L0_xattn_Wq', 'L0_xattn_bq', 'L0_xattn_Wk', 'L0_xattn_bk', 'L0_xattn_Wv', 'L0_xattn_bv',
        'L0_xattn_Wo', 'L0_xattn_bo', 'L0_ffn_w1', 'L0_ffn_s1', 'L0_ffn_w2', 'L0_ffn_s2', 'L0_ffn_w3', 'L0_ffn_s3']


def kernel(**inputs):
    import numpy as _np
    import concourse.bacc as _bacc
    from concourse import mybir as _mybir
    from concourse.bass_utils import run_bass_kernel_spmd as _run

    nc = _bacc.Bacc("TRN2", target_bir_lowering=False, num_devices=1)
    arrays, args = {}, []
    for name in _INS:
        a = _np.ascontiguousarray(inputs[name])
        arrays[f"in_{name}_dram"] = a
        args.append(nc.dram_tensor(f"in_{name}_dram", a.shape, _mybir.dt.from_np(a.dtype), kind="ExternalInput").ap())
    shape = inputs['x'].shape
    args.append(nc.dram_tensor("out_0_dram", shape, _mybir.dt.float32, kind="ExternalOutput").ap())
    bass_xattn_ffn_kernel(nc, *args)
    r = _run(nc, [arrays], core_ids=[0])
    return r.results[0]["out_0_dram"]
```

```python
import concourse.bass as bass
from concourse import mybir
from contextlib import ExitStack


def bass_xattn_ffn_kernel(nc, x, ctx_in, wq, bq, wk, bk, wv, bv, wo, bo, w1, s1, w2, s2, w3, s3, out):
    fp32, fp16, i32 = mybir.dt.float32, mybir.dt.float16, mybir.dt.int32
    ALU, ACT, AX = mybir.AluOpType, mybir.ActivationFunctionType, mybir.AxisListType

    B, D, L = x.shape
    P = 128
    H = 8
    LH = L // H
    HH = H // 2
    HL = HH * LH
    G = 64
    F = w1.shape[0] * 2 * G // L
    NT = -(-F // P)
    LAST = F - (NT - 1) * P
    K = L // P
    T = B * D
    TW = 512
    TS = T // TW
    TOK = TW // P
    YG = TOK * L // 512
    GT = TS * YG
    ROWG = F // G
    MB = L // (2 * P)
    EPS = 1e-5
    SCALE = float(LH) ** -0.5
    XS = 10
    WS = 11
    HSH = 13
    TINY = 2.0 ** -40
    WARM = 28

    with ExitStack() as stack:
        def sb(name, shape, dt):
            return stack.enter_context(nc.sbuf_tensor(name, shape, dt))

        def sem(name):
            return stack.enter_context(nc.semaphore(name))

        acc = sb("acc", [P, B, L], fp32)
        xT = sb("xT", [P, B, 2, K, D], fp16)
        shared = sb("shared", [P, 10 * L], fp32)
        w13_even = sb("w13_even", [P, 4 * L], fp16)
        raw = sb("raw", [P, 2, 12 * G], i32)
        q_int = sb("q_int", [P, 2, L], i32)
        w_nat16 = sb("w_nat16", [P, 2, 2, L], fp16)
        s1_sb = sb("s1_sb", [P, NT - 1, 2 * K], fp32)
        s3_sb = sb("s3_sb", [P, NT - 1, 2 * K], fp32)
        s31_sb = sb("s31_sb", [P, 2 * K], fp32)
        s2_sb = sb("s2_sb", [P, 2 * MB, ROWG + 1], fp32)
        ident = sb("ident", [P, P], fp32)
        ident16 = sb("ident16", [P, P], fp16)
        wT = sb("wT", [P, 4, P], fp32)
        bq_row = sb("bq_row", [P, P], fp32)
        bk_row = sb("bk_row", [P, P], fp32)
        bv_col = sb("bv_col", [P, 1], fp32)
        bo_col = sb("bo_col", [P, 1], fp32)
        neg_half = sb("neg_half", [P, 1], fp32)
        smax = sb("smax", [P, 3], fp32)
        smax31 = sb("smax31", [P, 1], fp32)
        smax_all = sb("smax_all", [P, 3], fp32)
        pow2 = sb("pow2", [P, 3], fp32)
        winv = sb("winv", [P, 3], fp32)
        prod = sb("prod", [P, 1], fp32)
        a_scale = sb("a_scale", [P, 1], fp32)
        h_scale = sb("h_scale", [P, 1], fp32)
        y_scale = sb("y_scale", [P, 1], fp32)
        stats1 = sb("stats1", [P, 2, 6], fp32)
        stats2 = sb("stats2", [P, 2, 6], fp32)
        mv1 = sb("mv1", [P, 2], fp32)
        mv2 = sb("mv2", [P, 2], fp32)
        ln1 = sb("ln1", [P, 2], fp32)
        ln2 = sb("ln2", [P, 2], fp32)
        rstd1 = sb("rstd1", [P, 1], fp32)
        rstd2 = sb("rstd2", [P, 1], fp32)
        nb1 = sb("nb1", [P, 1], fp32)
        nb2 = sb("nb2", [P, 1], fp32)
        gate_dve = sb("gate_dve", [P, 1], fp32)
        gate_pool = sb("gate_pool", [P, 1], fp32)
        nmax = sb("nmax", [P, H], fp32)
        rsum = sb("rsum", [P, H], fp32)
        rinv = sb("rinv", [P, H], fp32)

        def part(n, count, dt=fp32):
            view = shared[:, n * L:(n + count) * L]
            return view if dt is fp32 else view.bitcast(dt)

        ctx = [part(0, 1), part(1, 1)]
        vbuf = [part(2, 1), part(3, 1)]
        xn, qT, kT, prob, wop, x2 = (part(n, 1) for n in range(4, 10))
        x2_16 = xT[:, B - 1].rearrange("p h k s -> p (h k s)")
        turned = xT[:, B - 2].rearrange("p h k s -> p (h k s)")
        x2_16_last = part(1, 1, fp16)
        w_nat = part(9, 1)
        h_hi = [part(0, 1, fp16), part(1, 1, fp16)]
        h_lo = [part(2, 1, fp16), part(3, 1, fp16)]
        silu_sb = [part(4, 1)[:, 0:TW], part(4, 1)[:, TW:2 * TW]]
        h32 = [part(5, 1)[:, 0:TW], part(5, 1)[:, TW:2 * TW]]
        w13 = [w13_even[:, :], part(6, 2, fp16)]
        w2T = [part(8, 1, fp16), part(9, 1, fp16)]

        def w13_at(slot, which, half):
            o = (2 * which + half) * L
            return w13[slot][:, o:o + L]

        def w2_at(slot, half, odd):
            return w2T[slot][:, half * L:(half + 1) * L].rearrange("p (m r c) -> p r m c", m=MB, r=2)[:, odd]

        bank = [stack.enter_context(nc.psum_tensor(f"bank{n}", [P, 512], fp32)) for n in range(8)]
        q_ps, k_ps, v_ps, s_ps = bank[0:2], bank[2:4], bank[4:6], bank[6:8]
        proj_ps = [bank[6], bank[7], bank[0], bank[1]]
        wop_ps, y_ps = bank[4:6], bank[2:4]
        a_ps, b_ps, o_ps = [bank[0], bank[2]], [bank[1], bank[3]], bank[4:6]

        s_scales = sem("s_scales")
        proj_in = [sem(f"{w}_in") for w in ("wk", "wv", "wq", "wo")]
        s_bias_in = sem("s_bias_in")
        s_ident = sem("s_ident")
        s_projT = sem("s_projT")
        s_proj = sem("s_proj")
        s_bias = sem("s_bias")
        s_smax = sem("s_smax")
        s_smax31 = sem("s_smax31")
        s_smax_all = sem("s_smax_all")
        s_pow = sem("s_pow")
        s_sc = sem("s_sc")
        x_in = [sem("x_in0"), sem("x_in1")]
        c_in = [sem("c_in0"), sem("c_in1")]
        s_bn1, s_mv1, s_ln1, s_rstd1, s_xn = (sem(n) for n in ("s_bn1", "s_mv1", "s_ln1", "s_rstd1", "s_xn"))
        s_bn2, s_mv2, s_ln2, s_rstd2, s_x2 = (sem(n) for n in ("s_bn2", "s_mv2", "s_ln2", "s_rstd2", "s_x2"))
        s_nb1, s_nb2 = sem("s_nb1"), sem("s_nb2")
        s_q, s_k, s_v = sem("s_q"), sem("s_k"), sem("s_v")
        s_qe, s_ke, s_ve = sem("s_qe"), sem("s_ke"), sem("s_ve")
        s_score = sem("s_score")
        s_nmax = sem("s_nmax")
        s_exp = sem("s_exp")
        s_rinv = sem("s_rinv")
        s_prob = sem("s_prob")
        s_wop = sem("s_wop")
        s_wope = sem("s_wope")
        s_att = sem("s_att")
        s_res = sem("s_res")
        s_xhi, s_xlo = sem("s_xhi"), sem("s_xlo")
        s_turned = sem("s_turned")
        s_xT = sem("s_xT")
        raw_in = [sem("raw_in0"), sem("raw_in1")]
        s_unp = sem("s_unp")
        s_wf, s_whi, s_wlo = sem("s_wf"), sem("s_whi"), sem("s_wlo")
        s_turn = sem("s_turn")
        w_in = [sem("w1_in"), sem("w3_in"), sem("w2_in")]
        s_ab = sem("s_ab")
        s_silu, s_h, s_hhi, s_hlo = sem("s_silu"), sem("s_h"), sem("s_hhi"), sem("s_hlo")
        s_hlo_end = sem("s_hlo_end")
        s_y = sem("s_y")
        s_acc = sem("s_acc")
        s_out = sem("s_out")

        def after(eng, s, count):
            if not (type(count) is int and count <= 0):
                eng.wait_ge(s, count)

        def num(at):
            return 2 * at[0] + at[1]

        def nxt(at):
            return (at[0], 1) if at[1] == 0 else (at[0] + 1, 0)

        def prv(at):
            return (at[0], 0) if at[1] == 1 else (at[0] - 1, 1)

        END = ((NT - 1) // 2, 1)

        def is_end(at):
            return type(at[0]) is int and at == END

        def mat(at, m):
            if is_end(at) and m == 2:
                return 3 * NT - 2, 0, (3 * NT - 2) // 2
            return 3 * num(at) + m, (3 * at[1] + m) % 2, 3 * at[0] + (3 * at[1] + m) // 2

        w1_rows = w1.rearrange("(h c) j -> h c j", c=K)
        w3_rows = w3.rearrange("(h c) j -> h c j", c=K)
        w2_rows = w2.rearrange("(m p r) j -> p m r j", p=P, r=ROWG)

        block = stack.enter_context(nc.Block())

        @block.sync
        def _(sp):
            def load_batch(at):
                b = num(at)
                after(sp, s_mv1, b - 1)
                sp.dma_start(acc[:, bass.ds(b, 1), :], x[bass.ds(b, 1)].rearrange("b s l -> s b l")).then_inc(x_in[at[1]], 16)
                after(sp, s_v, 2 * (b - 1))
                sp.dma_start(ctx[at[1]], ctx_in[bass.ds(b, 1)].rearrange("b s l -> s (b l)")).then_inc(c_in[at[1]], 16)

            def load_weights(at, m):
                n, slot, _ = mat(at, m)
                i = num(at)
                dst = raw[:, slot, :]
                after(sp, s_unp, n - 1)
                if m < 2:
                    src = w1_rows if m == 0 else w3_rows
                    d = dst[:, 0:K * G].rearrange("p (c j) -> p c j", c=K)
                    half = K // 2
                    if is_end(at):
                        for rows, w in ((d[0:LAST], w3_rows), (d[LAST:P], w1_rows)):
                            sp.dma_start(rows, w[i * P:F]).then_inc(raw_in[slot], 16)
                    else:
                        for c in (0, half):
                            sp.dma_start(d[:, c:c + half, :], src[bass.ds(i * P, P), c:c + half, :]).then_inc(raw_in[slot], 16)
                else:
                    d = dst.rearrange("p (m r j) -> p m r j", m=MB, r=3)
                    first = ROWG // 2 + i
                    sp.dma_start(d[:, :, 0:1, :], w2_rows[:, :, bass.ds(i, 1), :]).then_inc(raw_in[slot], 16)
                    if is_end(at):
                        sp.dma_start(d[:, :, 1:2, :], w2_rows[:, :, first:first + 1, :]).then_inc(raw_in[slot], 16)
                    else:
                        sp.dma_start(d[:, :, 1:3, :], w2_rows[:, :, bass.ds(first, 2), :]).then_inc(raw_in[slot], 16)

            load_batch((0, 0))
            with nc.allow_non_contiguous_dma(reason="biases and scales, once"):
                for row, b in ((bk_row, bk), (bq_row, bq)):
                    sp.dma_start(row[:, :], b.rearrange("(a o) -> a o", a=1).to_broadcast([P, P])).then_inc(s_bias_in, 16)
                for col, b in ((bv_col, bv), (bo_col, bo)):
                    sp.dma_start(col[:, :], b.rearrange("(o a) -> o a", a=1)).then_inc(s_bias_in, 16)
                load_batch((0, 1))
                full = (NT - 1) * P
                for s, s_sb, half in ((s1, s1_sb, slice(LAST, P)), (s3, s3_sb, slice(0, LAST))):
                    rows = s.rearrange("(h g) -> h g", g=2 * K)
                    sp.dma_start(s_sb[:, :, :], rows[0:full].rearrange("(i p) g -> p i g", p=P)).then_inc(s_scales, 16)
                    sp.dma_start(s31_sb[half, :], rows[full:F]).then_inc(s_scales, 16)
                pairs = s2.rearrange("(m p r k) -> m p r k", p=P, r=2, k=ROWG)
                for m in range(MB):
                    sp.dma_start(s2_sb[:, 2 * m:2 * m + 2, 0:ROWG], pairs[m]).then_inc(s_scales, 16)
            load_weights((0, 0), 0)
            load_weights((0, 0), 1)
            with sp.Fori(1, B // 2) as u:
                load_batch((u, 0))
                load_batch((u, 1))
            load_weights((0, 0), 2)
            with sp.Fori(0, (NT - 2) // 2) as u:
                for at in ((u, 1), (u + 1, 0)):
                    for m in range(3):
                        load_weights(at, m)
            load_weights(END, 0)
            load_weights(END, 2)

            with sp.Fori(0, B) as b:
                sp.wait_ge(s_acc, 2 * b + GT * (NT - 2) + 2)
                sp.dma_start(out[bass.ds(b, 1)].rearrange("b s l -> s b l"), acc[:, bass.ds(b, 1), :]).then_inc(s_out, 16)
            sp.wait_ge(s_out, 16 * B)

        @block.gpsimd
        def _(pool):
            nc.gpsimd.memset(neg_half[:, :], -0.5)
            nc.gpsimd.memset(ident16[:, :], 0.0).then_inc(s_ident, 1)
            nc.gpsimd.memset(ident[:, :], 0.0).then_inc(s_ident, 1)
            pool.wait_ge(s_ident, 2)
            for m in (ident, ident16):
                nc.gpsimd.affine_select(out=m[:, :], in_=m[:, :], compare_op=ALU.not_equal, fill=1.0, base=0,
                                        pattern=[[-1, P]], channel_multiplier=1).then_inc(s_ident, 1)

            def gate():
                nc.gpsimd.tensor_tensor(gate_pool[:, :], neg_half[:, :], neg_half[:, :], ALU.add)

            def rstd(b, s_ln, ln, s_rstd, r, s_nb, nb, s_used):
                pool.wait_ge(s_ln, 2 * (b + 1))
                after(pool, s_used, b)
                nc.gpsimd.tensor_tensor(r[:, :], ln[:, 1:2], neg_half[:, :], ALU.pow).then_inc(s_rstd, 1)
                pool.wait_ge(s_rstd, b + 1)
                nc.gpsimd.tensor_tensor(nb[:, :], ln[:, 0:1], r[:, :], ALU.mult).then_inc(s_nb, 1)

            def rstd_1(at):
                rstd(num(at), s_ln1, ln1, s_rstd1, rstd1, s_nb1, nb1, s_xn)

            def rstd_2(at):
                rstd(num(at), s_ln2, ln2, s_rstd2, rstd2, s_nb2, nb2, s_x2)

            def scale_prob(at):
                b = num(at)
                for hf in range(2):
                    pool.wait_ge(s_rinv, 2 * b + hf + 1)
                    p = prob[:, hf * HL:(hf + 1) * HL].rearrange("p (h e) -> p h e", h=HH)
                    r = rinv[:, hf * HH:(hf + 1) * HH].unsqueeze(2).to_broadcast([P, HH, LH])
                    nc.gpsimd.tensor_tensor(p, p, r, ALU.mult).then_inc(s_prob, 1)

            def x_low(at, last=False):
                b = num(at)
                pool.wait_ge(s_xhi, b + 1)
                dst = (x2_16_last if last else x2_16)[:, L:2 * L]
                hi = (x2_16_last if last else x2_16)[:, 0:L]
                nc.gpsimd.tensor_tensor(dst, x2, hi, ALU.subtract).then_inc(s_xlo, 1)

            def att_step(at, first=False, ahead=True, first_tile=None):
                if not first:
                    rstd_2(prv(at))
                scale_prob(at)
                if ahead:
                    rstd_1(nxt(nxt(at)))
                if first_tile is not None:
                    split((0, 0), first_tile)
                if not first:
                    x_low(prv(at))

            def normalise_scales():
                pool.wait_ge(s_pow, 8)
                every = slice(0, P)
                for done, (s_sb, rows, n) in enumerate((
                        (s1_sb[:, :, :], every, 0), (s3_sb[:, :, :], every, 1), (s2_sb[:, :, 0:ROWG], every, 2),
                        (s31_sb[0:LAST, :], slice(0, LAST), 1), (s31_sb[LAST:P, :], slice(LAST, P), 0))):
                    if rows != every:
                        pool.wait_ge(s_sc, done)
                    nc.gpsimd.tensor_scalar(s_sb, s_sb, winv[rows, n:n + 1], 1.0, ALU.mult, ALU.mult).then_inc(s_sc, 1)
                pool.wait_ge(s_sc, 5)
                nc.gpsimd.tensor_scalar(s2_sb[:, :, ROWG:ROWG + 1], s2_sb[:, :, ROWG - 1:ROWG], 1.0, 1.0, ALU.mult, ALU.mult).then_inc(s_sc, 1)

            def split(at, m):
                n, slot, _ = mat(at, m)
                f = q_int[:, slot, :].bitcast(fp32)
                pool.wait_ge(s_wf, n + 1)
                before, tile = ((m + 1) % 3, num(at) + m // 2) if not is_end(at) or m < 2 else (2, num(at))
                after(pool, w_in[before], 16 * tile)
                gate()
                nc.gpsimd.tensor_scalar(w_nat16[:, slot, 0, :], f, 1.0, 1.0, ALU.mult, ALU.mult).then_inc(s_whi, 1)
                pool.wait_ge(s_whi, n + 1)
                nc.gpsimd.tensor_tensor(w_nat16[:, slot, 1, :], f, w_nat16[:, slot, 0, :], ALU.subtract).then_inc(s_wlo, 1)

            def h_low(at, t):
                n = TS * num(at) + t
                o = t * TW
                pool.wait_ge(s_hhi, n + 1)
                nc.gpsimd.tensor_tensor(h_lo[at[1]][:, o:o + TW], h32[t % 2], h_hi[at[1]][:, o:o + TW],
                                        ALU.subtract).then_inc(s_hlo, 1)

            def ffn_step(at):
                for t in range(TS):
                    if t < 3 and not (t == 1 and is_end(nxt(at))):
                        split(nxt(at), t)
                    h_low(at, t)

            rstd_1((0, 0))
            rstd_1((0, 1))
            att_step((0, 0), first=True)
            att_step((0, 1))
            pool.wait_ge(s_smax, 5)
            nc.gpsimd.partition_all_reduce(smax_all[:, :], smax[:, :], P, bass.bass_isa.ReduceOp.max).then_inc(s_smax_all, 1)
            att_step((1, 0))
            normalise_scales()
            att_step((1, 1))
            att_step((2, 0))
            att_step((2, 1), first_tile=0)
            att_step((3, 0), first_tile=1)
            att_step((3, 1))
            with pool.Fori(4, B // 2 - 1) as u:
                att_step((u, 0))
                att_step((u, 1))
            last = B // 2 - 1
            att_step((last, 0), ahead=False)
            att_step((last, 1), ahead=False, first_tile=2)
            rstd_2((last, 1))
            h_low((0, 0), 0)
            x_low((last, 1), last=True)
            h_low((0, 0), 1)
            split((0, 1), 0)
            h_low((0, 0), 2)
            split((0, 1), 1)
            h_low((0, 0), 3)
            split((0, 1), 2)
            ffn_step((0, 1))
            with pool.Fori(1, NT // 2 - 1) as u:
                ffn_step((u, 0))
                ffn_step((u, 1))
            ffn_step((NT // 2 - 1, 0))

        @block.scalar
        def _(act):
            def copy_v(at):
                b = num(at)
                for hf in range(2):
                    act.wait_ge(s_v, 2 * b + hf + 1)
                    after(act, s_att, 2 * (b - 1))
                    nc.scalar.activation(vbuf[at[1]][:, hf * HL:(hf + 1) * HL], v_ps[hf][:, :], ACT.Identity,
                                         bias=bv_col[:, 0:1]).then_inc(s_ve, 1)

            def exps(at):
                b = num(at)
                for h in range(H):
                    hf, o = h // HH, (h % HH) * LH
                    if h % HH == 0:
                        act.wait_ge(s_nmax, 2 * b + hf + 1)
                        after(act, s_wop, 2 * b)
                        after(act, s_rinv, 2 * b)
                    nc.scalar.activation(prob[:, h * LH:(h + 1) * LH], s_ps[hf][:, o:o + LH], ACT.Exp,
                                         bias=nmax[:, h:h + 1], accum_out=rsum[:, h:h + 1]).then_inc(s_exp, 1)

            def copy_wop(at):
                b = num(at)
                for hf in range(2):
                    act.wait_ge(s_wop, 2 * b + hf + 1)
                    after(act, s_att, 2 * b)
                    nc.scalar.activation(wop[:, hf * HL:(hf + 1) * HL], wop_ps[hf][:, :], ACT.Copy).then_inc(s_wope, 1)

            def x_high(at, last=False):
                b = num(at)
                act.wait_ge(s_x2, b + 1)
                after(act, s_turned, 16 * b)
                dst = (x2_16_last if last else x2_16)[:, 0:L]
                nc.scalar.activation(dst, x2, ACT.Copy).then_inc(s_xhi, 1)

            def turn_x(at, dst=turned, src=x2_16):
                b = num(at)
                act.wait_ge(s_xlo, b + 1)
                after(act, s_xT, 16 * min(b, B - 2) if type(b) is int else 16 * b)
                nc.scalar.sem_inc(s_turn, 1)
                act.dma_start(dst.rearrange("p (c s) -> p c s", s=D), src, transpose=True).then_inc(s_turned, 16)

            def place_xT(at):
                b = num(at)
                act.wait_ge(s_turned, 16 * (b + 1))
                act.dma_start(xT[:, bass.ds(b, 1)].rearrange("p b h k s -> p (b h k s)"), turned).then_inc(s_xT, 16)

            def norm(b, s_nb, nb, r, dst, s_free, used, s_done):
                after(act, s_free, used)
                act.wait_ge(s_nb, b + 1)
                nc.scalar.activation(dst, acc[:, bass.ds(b, 1), :].rearrange("p a l -> p (a l)"), ACT.Identity,
                                     bias=nb[:, 0:1], scale=r[:, 0:1]).then_inc(s_done, 1)

            def norm_1(at):
                norm(num(at), s_nb1, nb1, rstd1, xn, s_q, 2 * num(at), s_xn)

            def norm_2(at):
                norm(num(at), s_nb2, nb2, rstd2, x2, s_xlo, num(at), s_x2)

            def att_step(at, first=False, second=True, ahead=True, first_weights=False):
                exps(at)
                if second:
                    turn_x(prv(prv(at)))
                copy_v(nxt(at))
                if not first:
                    norm_2(prv(at))
                copy_wop(at)
                if first_weights:
                    weight_slot((0, 0), 0)
                    weight_slot((0, 0), 1)
                if second:
                    place_xT(prv(prv(at)))
                if not first:
                    x_high(prv(at))
                if ahead:
                    norm_1(nxt(nxt(at)))

            def weight_slot(at, m):
                n, slot, _ = mat(at, m)
                i = num(at)
                if m < 2:
                    after(act, s_ab, TS * (i - 1))
                    dst = w13[at[1]][:, 2 * m * L:2 * (m + 1) * L]
                else:
                    after(act, s_y, GT * (i - 1))
                    dst = w2T[at[1]]
                act.wait_ge(s_wlo, n + 1)
                nc.scalar.sem_inc(s_turn, 1)
                act.dma_start(dst.rearrange("p (c r) -> p c r", r=P), w_nat16[:, slot, :, :].rearrange("p h l -> p (h l)"),
                              transpose=True).then_inc(w_in[m], 16)

            def silu(at, t):
                n = TS * num(at) + t
                act.wait_ge(s_ab, n + 1)
                after(act, s_h, n - 1)
                if is_end(at):
                    nc.scalar.activation(silu_sb[t % 2][0:LAST], a_ps[t % 2][LAST:P, :], ACT.Silu,
                                         scale=a_scale[LAST:P, 0:1]).then_inc(s_silu, 1)
                else:
                    nc.scalar.activation(silu_sb[t % 2], a_ps[t % 2][:, :], ACT.Silu, scale=a_scale[:, 0:1]).then_inc(s_silu, 1)

            def h_high(at, t):
                rows = slice(0, LAST if is_end(at) else P)
                act.wait_ge(s_h, TS * num(at) + t + 1)
                after(act, s_y, GT * (num(at) - 1))
                nc.scalar.activation(h_hi[at[1]][rows, t * TW:(t + 1) * TW], h32[t % 2][rows], ACT.Copy).then_inc(s_hhi, 1)

            def ffn_step(at):
                for t in range(TS):
                    silu(at, t)
                    if t == 0:
                        weight_slot(at, 2)
                    elif t < 3 and not is_end(at) and not (t == 2 and is_end(nxt(at))):
                        weight_slot(nxt(at), t - 1)
                    h_high(at, t)

            def copy_proj(n):
                act.wait_ge(s_projT, n + 1)
                nc.scalar.activation(wT[:, n, :], proj_ps[n][:, 0:P], ACT.Copy).then_inc(s_proj, 1)

            for n, w in enumerate((wk, wv, wq, wo)):
                act.dma_start(w_nat[:, n * P:(n + 1) * P], w).then_inc(proj_in[n], 16)
            copy_proj(0)
            copy_proj(1)
            norm_1((0, 0))
            copy_proj(2)
            copy_proj(3)
            act.wait_ge(s_bias_in, 16 * 4)
            copy_v((0, 0))
            norm_1((0, 1))
            att_step((0, 0), first=True, second=False)
            att_step((0, 1), second=False)
            att_step((1, 0))
            att_step((1, 1))
            with act.Fori(2, B // 2 - 1) as u:
                att_step((u, 0))
                att_step((u, 1))
            last = B // 2 - 1
            att_step((last, 0), ahead=False, first_weights=True)
            exps((last, 1))
            turn_x((last - 1, 1))
            norm_2((last, 0))
            place_xT((last - 1, 1))
            x_high((last, 0))
            copy_wop((last, 1))
            act.wait_ge(s_pow, 8)
            silu((0, 0), 0)
            h_high((0, 0), 0)
            turn_x((last, 0))
            norm_2((last, 1))
            silu((0, 0), 1)
            x_high((last, 1), last=True)
            h_high((0, 0), 1)
            turn_x((last, 1), dst=x2_16, src=x2_16_last)
            act.wait_ge(s_att, 2 * B)
            weight_slot((0, 0), 2)
            silu((0, 0), 2)
            weight_slot((0, 1), 0)
            h_high((0, 0), 2)
            weight_slot((0, 1), 1)
            silu((0, 0), 3)
            h_high((0, 0), 3)
            ffn_step((0, 1))
            with act.Fori(1, NT // 2 - 1) as u:
                ffn_step((u, 0))
                ffn_step((u, 1))
            ffn_step((NT // 2 - 1, 0))
            ffn_step(END)

        @block.tensor
        def _(pe):
            def cols(n, w=P):
                return slice(n * w, (n + 1) * w)

            def project_k(at, halves=(0, 1)):
                b = num(at)
                pe.wait_ge(c_in[at[1]], 16 * (at[0] + 1))
                for hf in halves:
                    after(pe, s_res, 2 * (b - 2) + hf + 1)
                    for h in range(HH):
                        mm = nc.tensor.matmul(k_ps[hf][:, cols(h)], ctx[at[1]][:, cols(hf * HH + h)], wT[:, 0, :], start=True, stop=True)
                    mm.then_inc(s_k, 1)

            def project_vq(at):
                b = num(at)
                for hf in range(2):
                    after(pe, s_ve, 2 * (b - 1) + hf + 1)
                    after(pe, s_wope, 2 * (b - 2) + hf + 1)
                    nc.tensor.matmul(v_ps[hf][:, :], wT[:, 1, :], ctx[at[1]][:, cols(hf, HL)], start=True, stop=True).then_inc(s_v, 1)
                pe.wait_ge(s_xn, b + 1)
                for hf in range(2):
                    for h in range(HH):
                        mm = nc.tensor.matmul(q_ps[hf][:, cols(h)], xn[:, cols(hf * HH + h)], wT[:, 2, :], start=True, stop=True)
                    mm.then_inc(s_q, 1)

            def scores(at):
                b = num(at)
                for hf in range(2):
                    pe.wait_ge(s_qe, 2 * b + hf + 1)
                    pe.wait_ge(s_ke, 2 * b + hf + 1)
                    after(pe, s_exp, H * (b - 1) + HH * (hf + 1))
                    for h in range(HH):
                        c = cols(hf * HH + h)
                        mm = nc.tensor.matmul(s_ps[hf][:, cols(h)], qT[:, c], kT[:, c], start=True, stop=True)
                    mm.then_inc(s_score, 1)

            def wo_prob(at, last):
                b = num(at)
                for hf in range(2):
                    pe.wait_ge(s_prob, 2 * b + hf + 1)
                    if not last:
                        pe.wait_ge(s_ve, 2 * (b + 1) + hf + 1)
                    for h in range(HH):
                        mm = nc.tensor.matmul(wop_ps[hf][:, cols(h)], prob[:, cols(hf * HH + h)], wT[:, 3, :], start=True, stop=True)
                    mm.then_inc(s_wop, 1)

            def attend(at, last, ps=y_ps):
                b = num(at)
                for hf in range(2):
                    pe.wait_ge(s_wope, 2 * b + hf + 1)
                    pe.wait_ge(s_ve, 2 * b + hf + 1)
                    if not last:
                        pe.wait_ge(s_ke, 2 * (b + 1) + hf + 1)
                    for h in range(HH):
                        c = cols(hf * HH + h)
                        mm = nc.tensor.matmul(ps[hf][:, cols(h)], wop[:, c], vbuf[at[1]][:, c], start=True, stop=True)
                    mm.then_inc(s_att, 1)

            def att_step(at):
                scores(at)
                project_k(nxt(at))
                project_vq(nxt(at))
                wo_prob(at, last=False)
                attend(at, last=False)

            def product(dst, w_hi, w_lo, t, k):
                dst = dst[:, :].rearrange("p (b s) -> p b s", s=D)
                x_hi, x_lo = (xT[:, t * TOK:(t + 1) * TOK, half, k, :] for half in range(2))
                nc.tensor.matmul(dst, w_hi, x_hi, start=(k == 0), stop=False)
                nc.tensor.matmul(dst, w_hi, x_lo, start=False, stop=False)
                return nc.tensor.matmul(dst, w_lo, x_hi, start=False, stop=(k == K - 1))

            def gate_up(at, t, piece):
                n = TS * num(at) + t
                m, part_of = piece // 4, piece % 4
                dst = (a_ps, b_ps)[m][t % 2]
                if t == 0 and part_of == 0:
                    pe.wait_ge(w_in[m], 16 * (num(at) + 1))
                if piece == 0:
                    after(pe, s_h, n - 1)
                for k in range(2 * part_of, 2 * part_of + 2):
                    mm = product(dst, w13_at(at[1], m, 0)[:, cols(k)], w13_at(at[1], m, 1)[:, cols(k)], t, k)
                if piece == 7:
                    mm.then_inc(s_ab, 1)

            def down(at, t, g, and_last=False):
                n = GT * num(at) + YG * t + g
                if t == 0 and g == 0:
                    pe.wait_ge(w_in[2], 16 * (num(at) + 1))
                if g == 0:
                    pe.wait_ge(s_hlo, TS * num(at) + t + 1)
                    if and_last:
                        pe.wait_ge(s_hlo_end, t + 1)
                after(pe, s_acc, n if t == g == 0 else n - 1)
                tok, odd = cols(t * TOK + g // 2), g % 2
                dst = o_ps[g % 2][:, :].rearrange("p (m c) -> p m c", m=MB)
                hi, lo = h_hi[at[1]], h_lo[at[1]]
                nc.tensor.matmul(dst, hi[:, tok], w2_at(at[1], 0, odd), start=True, stop=False)
                nc.tensor.matmul(dst, hi[:, tok], w2_at(at[1], 1, odd), start=False, stop=False)
                mm = nc.tensor.matmul(dst, lo[:, tok], w2_at(at[1], 0, odd), start=False, stop=not and_last)
                if and_last:
                    if t == 0 and g == 0:
                        pe.wait_ge(w_in[2], 16 * NT)
                    nc.tensor.matmul(dst, h_hi[1][:, tok], w2_at(1, 0, odd), start=False, stop=False)
                    mm = nc.tensor.matmul(dst, h_hi[1][0:LAST, tok], w2_at(1, 1, odd)[0:LAST], start=False, stop=True)
                mm.then_inc(s_y, 1)

            def gate_up_end(t, k):
                if t == 0 and k == 0:
                    pe.wait_ge(w_in[0], 16 * NT)
                if k == 0:
                    pe.wait_ge(s_h, TS * (NT - 1) + t - 1)
                mm = product(a_ps[t % 2], w13_at(1, 0, 0)[:, cols(k)], w13_at(1, 0, 1)[:, cols(k)], t, k)
                if k == K - 1:
                    mm.then_inc(s_ab, 1)

            def ffn_step(at):
                for t in range(TS):
                    for piece in range(8):
                        gate_up(at, t, piece)
                        down(prv(at), t, piece)

            def gate_up_all(at, t):
                pe.wait_ge(s_xT, 16 * min(TOK * (t + 1), B - 2))
                if t == TS - 1:
                    pe.wait_ge(s_turned, 16 * B)
                for piece in range(8):
                    gate_up(at, t, piece)

            def warm(count):
                for n in range(count):
                    nc.tensor.matmul(bank[5][:, cols(n % 4)], ident16[:, :], ident16[:, :], start=True, stop=True)

            def turn_proj(n):
                pe.wait_ge(proj_in[n], 16)
                nc.tensor.transpose(proj_ps[n][:, 0:P], w_nat[:, cols(n)], ident[:, :]).then_inc(s_projT, 1)

            pe.wait_ge(s_ident, 4)
            warm(WARM)
            turn_proj(0)
            warm(WARM // 2)
            turn_proj(1)
            pe.wait_ge(s_proj, 1)
            project_k((0, 0), halves=(0,))
            turn_proj(2)
            turn_proj(3)
            project_k((0, 0), halves=(1,))
            pe.wait_ge(s_proj, 4)
            project_vq((0, 0))
            att_step((0, 0))
            att_step((0, 1))
            with pe.Fori(1, B // 2 - 1) as u:
                att_step((u, 0))
                att_step((u, 1))
            last = B // 2 - 1
            att_step((last, 0))
            scores((last, 1))
            gate_up_all((0, 0), 0)
            wo_prob((last, 1), last=True)
            attend((last, 1), last=True, ps=bank[6:8])
            pe.wait_ge(s_res, 2 * (B - 1))
            gate_up_all((0, 0), 1)
            gate_up_all((0, 0), 2)
            gate_up_all((0, 0), 3)
            ffn_step((0, 1))
            with pe.Fori(1, NT // 2 - 1) as u:
                ffn_step((u, 0))
                ffn_step((u, 1))
            ffn_step((NT // 2 - 1, 0))
            for t in range(TS + 2):
                for piece in range(YG):
                    if t < TS:
                        gate_up_end(t, piece)
                    if t >= 2:
                        down(prv(END), t - 2, piece, and_last=True)

        @block.vector
        def _(dve):
            def gate():
                nc.vector.memset(gate_dve[:, :], 0.0)

            def stats(b, src, st, mv, ln, s_bn, s_mv, s_ln, scale):
                gate()
                for hf in range(2):
                    nc.vector.bn_stats(st[:, hf, :], src[:, hf * 512:(hf + 1) * 512]).then_inc(s_bn, 1)
                dve.wait_ge(s_bn, 2 * (b + 1))
                gate()
                nc.vector.bn_aggr(mv[:, :], st[:, :, :]).then_inc(s_mv, 1)
                dve.wait_ge(s_mv, b + 1)
                nc.vector.tensor_scalar(ln[:, 0:1], mv[:, 0:1], -1.0, None, ALU.mult).then_inc(s_ln, 1)
                nc.vector.tensor_scalar(ln[:, 1:2], mv[:, 1:2], EPS, scale, ALU.add, ALU.mult).then_inc(s_ln, 1)

            def x_row(b):
                return acc[:, bass.ds(b, 1), :].rearrange("p a l -> p (a l)")

            def stats_1(at):
                b = num(at)
                dve.wait_ge(x_in[at[1]], 16 * (at[0] + 1))
                after(dve, s_nb1, b)
                stats(b, x_row(b), stats1, mv1, ln1, s_bn1, s_mv1, s_ln1, 1.0)

            def stats_2(at):
                b = num(at)
                dve.wait_ge(s_res, 2 * (b + 1))
                after(dve, s_nb2, b)
                stats(b, x_row(b), stats2, mv2, ln2, s_bn2, s_mv2, s_ln2, 2.0 ** (-2 * XS))

            def copy_q(at, hf):
                b = num(at)
                dve.wait_ge(s_q, 2 * b + hf + 1)
                bias = bq_row[:, :].unsqueeze(1).to_broadcast([P, HH, P])
                nc.vector.scalar_tensor_tensor(out=qT[:, hf * HL:(hf + 1) * HL].rearrange("p (h o) -> p h o", h=HH),
                                               in0=q_ps[hf][:, :].rearrange("p (h o) -> p h o", h=HH), scalar=SCALE,
                                               in1=bias, op0=ALU.mult, op1=ALU.add).then_inc(s_qe, 1)

            def copy_k(at, hf):
                b = num(at)
                dve.wait_ge(s_k, 2 * b + hf + 1)
                bias = bk_row[:, :].unsqueeze(1).to_broadcast([P, HH, P])
                nc.vector.tensor_tensor(kT[:, hf * HL:(hf + 1) * HL].rearrange("p (h o) -> p h o", h=HH),
                                        k_ps[hf][:, :].rearrange("p (h o) -> p h o", h=HH), bias, ALU.add).then_inc(s_ke, 1)

            def maxes(at):
                b = num(at)
                for hf in range(2):
                    dve.wait_ge(s_score, 2 * b + hf + 1)
                    after(dve, s_exp, H * b)
                    nc.vector.tensor_reduce(nmax[:, hf * HH:(hf + 1) * HH], s_ps[hf][:, :].rearrange("p (h e) -> p h e", h=HH),
                                            AX.X, ALU.max, negate=True).then_inc(s_nmax, 1)

            def invert(at, hf):
                b = num(at)
                dve.wait_ge(s_exp, H * b + HH * (hf + 1))
                after(dve, s_prob, 2 * b)
                nc.vector.reciprocal(rinv[:, hf * HH:(hf + 1) * HH], rsum[:, hf * HH:(hf + 1) * HH]).then_inc(s_rinv, 1)

            def residual(at, ps=y_ps):
                b = num(at)
                for hf in range(2):
                    dve.wait_ge(s_att, 2 * b + hf + 1)
                    after(dve, s_xn, b + 1)
                    xs = x_row(b)[:, hf * HL:(hf + 1) * HL]
                    nc.vector.scalar_tensor_tensor(out=xs, in0=ps[hf][:, :], scalar=bo_col[:, 0:1], in1=xs,
                                                   op0=ALU.add, op1=ALU.add).then_inc(s_res, 1)

            def att_step(at, first=False, ahead=True, between=None):
                maxes(at)
                if not first:
                    stats_2(prv(at))
                for hf in range(2):
                    invert(at, hf)
                    copy_k(nxt(at), hf)
                if ahead:
                    stats_1(nxt(nxt(at)))
                for hf in range(2):
                    copy_q(nxt(at), hf)
                if between:
                    between()
                residual(at)

            def unpack(at, m):
                n, slot, nth = mat(at, m)
                i = num(at)
                dve.wait_ge(raw_in[slot], 32 * (nth + 1))
                after(dve, s_wlo, n - 1)
                if m < 2:
                    src = raw[:, slot, 0:K * G].rearrange("p (c j) -> p c j", c=K)
                    dst = q_int[:, slot, :].rearrange("p (c e j) -> p c e j", c=K, e=2)
                    high, low, high_src, low_src = dst[:, :, 0, :], dst[:, :, 1, :], src, src
                elif is_end(at):
                    src = raw[:, slot, :].rearrange("p (m r j) -> p m r j", m=MB, r=3)
                    dst = q_int[:, slot, :].rearrange("p (m e j) -> p m e j", m=MB, e=4)
                    high, high_src = dst[:, :, 0:2, :], src[:, :, 0:1, :].to_broadcast([P, MB, 2, G])
                    low, low_src = dst[:, :, 2:4, :], src[:, :, 1:2, :].to_broadcast([P, MB, 2, G])
                else:
                    src = raw[:, slot, :].rearrange("p (m r j) -> p m r j", m=MB, r=3)
                    dst = q_int[:, slot, :].rearrange("p (m e j) -> p m e j", m=MB, e=4)
                    high, high_src = dst[:, :, 0:4:3, :], src[:, :, 0:3:2, :]
                    low, low_src = dst[:, :, 1:3, :], src[:, :, 0:2, :]
                nc.vector.tensor_scalar(high, high_src, 4, None, ALU.arith_shift_right)
                nc.vector.tensor_scalar(low, low_src, 28, 28, ALU.logical_shift_left, ALU.arith_shift_right).then_inc(s_unp, 1)

            def scale_weights(at, m):
                n, slot, _ = mat(at, m)
                i = num(at)
                view = "p (r g j) -> p r g j"
                r = 1 if m < 2 else 2 * MB
                q = q_int[:, slot, :].rearrange(view, r=r, j=G)
                w = q_int[:, slot, :].bitcast(fp32).rearrange(view, r=r, j=G)
                if m == 2:
                    s = s2_sb[:, :, bass.ds(2 * i, 2)]
                else:
                    s = s31_sb[:, :].unsqueeze(1) if is_end(at) else (s1_sb, s3_sb)[m][:, bass.ds(i, 1), :]
                s = s.unsqueeze(3).to_broadcast([P, r, q.shape[2], G])
                dve.wait_ge(s_unp, n + 1)
                nc.vector.tensor_tensor(w, q, s, ALU.mult).then_inc(s_wf, 1)

            def weights(at, m):
                unpack(at, m)
                scale_weights(at, m)

            def make_h(at, t):
                n = TS * num(at) + t
                dve.wait_ge(s_silu, n + 1)
                after(dve, s_hlo, n - 1)
                nc.vector.scalar_tensor_tensor(out=h32[t % 2], in0=b_ps[t % 2][:, :], scalar=h_scale[:, 0:1],
                                               in1=silu_sb[t % 2], op0=ALU.mult, op1=ALU.mult).then_inc(s_h, 1)

            def add_y(at, t, g):
                n = GT * num(at) + YG * t + g
                dve.wait_ge(s_y, n + 1)
                a = acc[:, t * TOK + g // 2, :].rearrange("p (m c r) -> p r m c", m=MB, r=2)[:, g % 2]
                y = o_ps[g % 2][:, :].rearrange("p (m c) -> p m c", m=MB)
                nc.vector.scalar_tensor_tensor(out=a, in0=y, scalar=y_scale[:, 0:1], in1=a,
                                               op0=ALU.mult, op1=ALU.add).then_inc(s_acc, 1)

            def make_h_end(t):
                n = TS * (NT - 1) + t
                dve.wait_ge(s_silu, n + 1)
                if t < 2:
                    dve.wait_ge(s_hlo, n - 1)
                else:
                    dve.wait_ge(s_hlo_end, t - 1)
                nc.vector.scalar_tensor_tensor(out=h32[t % 2][0:LAST], in0=a_ps[t % 2][0:LAST, :], scalar=h_scale[0:LAST, 0:1],
                                               in1=silu_sb[t % 2][0:LAST], op0=ALU.mult, op1=ALU.mult).then_inc(s_h, 1)

            def h_low_end(t):
                tok = slice(t * TW, (t + 1) * TW)
                dve.wait_ge(s_hhi, TS * (NT - 1) + t + 1)
                nc.vector.tensor_tensor(h_hi[1][LAST:P, tok], h32[t % 2][0:LAST], h_hi[1][0:LAST, tok],
                                        ALU.subtract).then_inc(s_hlo_end, 1)

            def ffn_step(at):
                for t in range(TS):
                    if t < 3 and not (t == 1 and is_end(nxt(at))):
                        weights(nxt(at), t)
                    for g in range(YG):
                        add_y(prv(at), t, g)
                    make_h(at, t)

            def largest_scales():
                dve.wait_ge(s_scales, 16 * (4 + MB))
                for n, s_sb in enumerate((s1_sb[:, :, :], s3_sb[:, :, :])):
                    nc.vector.tensor_reduce(smax[:, n:n + 1], s_sb, AX.XY, ALU.max, apply_absolute_value=True).then_inc(s_smax, 1)

            def largest_scales_2():
                nc.vector.tensor_reduce(smax[:, 2:3], s2_sb[:, :, 0:ROWG], AX.XY, ALU.max, apply_absolute_value=True).then_inc(s_smax, 1)
                nc.vector.tensor_reduce(smax31[:, :], s31_sb[:, :], AX.X, ALU.max, apply_absolute_value=True).then_inc(s_smax31, 1)
                dve.wait_ge(s_smax31, 1)
                dve.wait_ge(s_smax, 3)
                for n, rows in ((0, slice(LAST, P)), (1, slice(0, LAST))):
                    nc.vector.tensor_tensor(smax[rows, n:n + 1], smax[rows, n:n + 1], smax31[rows, :], ALU.max).then_inc(s_smax, 1)

            def powers():
                dve.wait_ge(s_smax_all, 1)
                nc.vector.tensor_scalar(smax_all[:, :], smax_all[:, :], TINY, None, ALU.max).then_inc(s_pow, 1)
                dve.wait_ge(s_pow, 1)
                nc.vector.tensor_scalar(pow2[:, :].bitcast(i32), smax_all[:, :].bitcast(i32), 0x7F800000, None,
                                        ALU.bitwise_and).then_inc(s_pow, 1)
                dve.wait_ge(s_pow, 2)
                nc.vector.reciprocal(winv[:, :], pow2[:, :]).then_inc(s_pow, 1)
                dve.wait_ge(s_pow, 3)
                nc.vector.tensor_scalar(a_scale[:, :], pow2[:, 0:1], 2.0 ** -(XS + WS), None, ALU.mult).then_inc(s_pow, 1)
                nc.vector.tensor_scalar(h_scale[:, :], winv[:, 0:1], 2.0 ** -(XS + WS + HSH), None, ALU.mult).then_inc(s_pow, 1)
                nc.vector.tensor_scalar(prod[:, :], pow2[:, 0:1], pow2[:, 1:2], 2.0 ** (HSH - WS), ALU.mult, ALU.mult).then_inc(s_pow, 1)
                dve.wait_ge(s_pow, 6)
                nc.vector.tensor_scalar(y_scale[:, :], prod[:, :], pow2[:, 2:3], None, ALU.mult).then_inc(s_pow, 1)
                nc.vector.tensor_scalar(winv[:, :], winv[:, :], 2.0 ** WS, None, ALU.mult).then_inc(s_pow, 1)

            def scale_first():
                dve.wait_ge(s_sc, 6)
                scale_weights((0, 0), 0)

            stats_1((0, 0))
            dve.wait_ge(s_bias_in, 16 * 4)
            nc.vector.tensor_scalar(bq_row[:, :], bq_row[:, :], SCALE, None, ALU.mult).then_inc(s_bias, 1)
            for hf in range(2):
                copy_k((0, 0), hf)
            stats_1((0, 1))
            dve.wait_ge(s_bias, 1)
            for hf in range(2):
                copy_q((0, 0), hf)
            att_step((0, 0), first=True, between=largest_scales)
            att_step((0, 1), between=largest_scales_2)
            att_step((1, 0), between=powers)
            att_step((1, 1), between=lambda: unpack((0, 0), 0))
            att_step((2, 0), between=scale_first)
            att_step((2, 1), between=lambda: weights((0, 0), 1))
            with dve.Fori(3, B // 2 - 1) as u:
                att_step((u, 0))
                att_step((u, 1))
            last = B // 2 - 1
            att_step((last, 0), ahead=False)
            maxes((last, 1))
            stats_2((last, 0))
            invert((last, 1), 0)
            invert((last, 1), 1)
            weights((0, 0), 2)
            residual((last, 1), ps=bank[6:8])
            stats_2((last, 1))
            make_h((0, 0), 0)
            weights((0, 1), 0)
            make_h((0, 0), 1)
            weights((0, 1), 1)
            make_h((0, 0), 2)
            weights((0, 1), 2)
            make_h((0, 0), 3)
            ffn_step((0, 1))
            with dve.Fori(1, NT // 2 - 1) as u:
                ffn_step((u, 0))
                ffn_step((u, 1))
            ffn_step((NT // 2 - 1, 0))
            for t in range(TS + 2):
                for g in range(YG):
                    if g == 1 and 1 <= t <= TS:
                        h_low_end(t - 1)
                    if t >= 2:
                        add_y(prv(END), t - 2, g)
                if t < TS:
                    make_h_end(t)


_INS = ['x', 'ctx_4096', 'L0_xattn_Wq', 'L0_xattn_bq', 'L0_xattn_Wk', 'L0_xattn_bk', 'L0_xattn_Wv', 'L0_xattn_bv',
        'L0_xattn_Wo', 'L0_xattn_bo', 'L0_ffn_w1', 'L0_ffn_s1', 'L0_ffn_w2', 'L0_ffn_s2', 'L0_ffn_w3', 'L0_ffn_s3']


def kernel(**inputs):
    import numpy as _np
    import concourse.bacc as _bacc
    from concourse import mybir as _mybir
    from concourse.bass_utils import run_bass_kernel_spmd as _run

    nc = _bacc.Bacc("TRN2", target_bir_lowering=False, num_devices=1)
    arrays, args = {}, []
    for name in _INS:
        a = _np.ascontiguousarray(inputs[name])
        arrays[f"in_{name}_dram"] = a
        args.append(nc.dram_tensor(f"in_{name}_dram", a.shape, _mybir.dt.from_np(a.dtype), kind="ExternalInput").ap())
    shape = inputs['x'].shape
    args.append(nc.dram_tensor("out_0_dram", shape, _mybir.dt.float32, kind="ExternalOutput").ap())
    bass_xattn_ffn_kernel(nc, *args)
    r = _run(nc, [arrays], core_ids=[0])
    return r.results[0]["out_0_dram"]
```
